# Optimizing a Trainium2 kernel written in Bass

```python
import numpy as np
import jax
import jax.numpy as jnp

def _softmax(x, axis=-1):
    return jax.nn.softmax(x, axis=axis)

def _gelu(x):
    return jax.nn.gelu(x, approximate=True)

def _silu(x):
    return jax.nn.silu(x)

def _sigmoid(x):
    return jax.nn.sigmoid(x)

def _layernorm(x, axis=-1, eps=1e-05):
    m = jnp.mean(x, axis=axis, keepdims=True)
    v = jnp.var(x, axis=axis, keepdims=True)
    return (x - m) / jnp.sqrt(v + eps)

def _scatter_add(tgt, idx, src, axis=0):
    return tgt.at[idx].add(src)

def _segment_sum(src, seg, n):
    return jax.ops.segment_sum(src, seg, n)
kernel_name = 'mk_adaln_d1_jaxref_r4_2ade34'

def setup_inputs(seed: int=0):
    np.random.seed(seed)
    _w = jnp.asarray

    def _L0_attn_setup():
        import jax, jax.numpy as jnp
        import numpy as np
        B, T, D, H, NT = (2, 512, 256, 16, 7)
        HD = D // H
        TEMP = 0.5
        key = jax.random.key(seed)
        ks = jax.random.split(key, 6)
        x = jax.random.normal(ks[0], (B, T, D), jnp.float32)
        qkv_w = jax.random.normal(ks[1], (3 * D, D), jnp.float32) / np.sqrt(D)
        out_w = jax.random.normal(ks[2], (D, D), jnp.float32) / np.sqrt(D)
        hex_w = jax.random.normal(ks[3], (6, D), jnp.float32) * 0.02
        q6_w = jax.random.normal(ks[4], (6, D), jnp.float32) * 0.02
        tr = np.zeros((NT, 6, 6), dtype=np.float32)
        for i in range(6):
            tr[i] = np.eye(6)
            tr[i, i, i] = -1.0
        tr[6] = -np.eye(6)
        transforms = jnp.asarray(tr)
        transform_weights = jax.random.normal(ks[5], (H, NT), jnp.float32) * 0.01
        hamming_lambda_logit = jnp.asarray(np.log(0.1 / 0.9), jnp.float32)
        scale_logit = jnp.zeros((), jnp.float32)
        sips_alpha = jnp.ones((1,), jnp.float32)
        sips_beta = jnp.full((1,), np.sqrt(HD), jnp.float32)
        return {'x': x, 'qkv_w': qkv_w, 'out_w': out_w, 'hex_w': hex_w, 'hamming_lambda_logit': hamming_lambda_logit, 'q6_w': q6_w, 'transforms': transforms, 'transform_weights': transform_weights, 'scale_logit': scale_logit, 'sips_alpha': sips_alpha, 'sips_beta': sips_beta}
    _L0_attn_in = _L0_attn_setup()

    def _L0_ffn_setup():
        import jax, jax.numpy as jnp
        import numpy as np
        EMB, HID, E, TOPK = (256, 1024, 8, 2)
        key = jax.random.key(seed)
        ks = jax.random.split(key, 10)
        s = 0.02
        return {'x': jax.random.normal(ks[0], (4, 512, EMB), jnp.float32), 'rw1': s * jax.random.normal(ks[1], (EMB, HID), jnp.float32), 'rb1': jnp.zeros((HID,), jnp.float32), 'rw2': s * jax.random.normal(ks[2], (HID, E), jnp.float32), 'rb2': jnp.zeros((E,), jnp.float32), 'w1': s * jax.random.normal(ks[3], (E, EMB, HID), jnp.float32), 'b1': jnp.zeros((E, HID), jnp.float32), 'w2': s * jax.random.normal(ks[4], (E, HID, EMB), jnp.float32), 'b2': jnp.zeros((E, EMB), jnp.float32)}
    _L0_ffn_in = _L0_ffn_setup()
    _L0_c = _w((lambda *s: np.random.randn(*s).astype(np.float32) * 0.05)(2, 256))
    _L0_wmod = _w((lambda *s: np.random.randn(*s).astype(np.float32) * 0.05)(256, 6 * 256) * 256 ** (-0.5))
    _d = {'L0_attn_x': _L0_attn_in['x'], 'L0_attn_qkv_w': _L0_attn_in['qkv_w'], 'L0_attn_out_w': _L0_attn_in['out_w'], 'L0_attn_hex_w': _L0_attn_in['hex_w'], 'L0_attn_hamming_lambda_logit': _L0_attn_in['hamming_lambda_logit'], 'L0_attn_q6_w': _L0_attn_in['q6_w'], 'L0_attn_transforms': _L0_attn_in['transforms'], 'L0_attn_transform_weights': _L0_attn_in['transform_weights'], 'L0_attn_scale_logit': _L0_attn_in['scale_logit'], 'L0_attn_sips_alpha': _L0_attn_in['sips_alpha'], 'L0_attn_sips_beta': _L0_attn_in['sips_beta'], 'L0_ffn_rw1': _L0_ffn_in['rw1'], 'L0_ffn_rb1': _L0_ffn_in['rb1'], 'L0_ffn_rw2': _L0_ffn_in['rw2'], 'L0_ffn_rb2': _L0_ffn_in['rb2'], 'L0_ffn_w1': _L0_ffn_in['w1'], 'L0_ffn_b1': _L0_ffn_in['b1'], 'L0_ffn_w2': _L0_ffn_in['w2'], 'L0_ffn_b2': _L0_ffn_in['b2'], 'L0_c': _L0_c, 'L0_wmod': _L0_wmod}
    _x0 = _d['L0_attn_x']
    _d['L0_attn_x'] = jax.random.normal(jax.random.fold_in(jax.random.key(seed), 1), (2, 2048, 256), dtype=_x0.dtype)
    del _x0
    return _d

def reference(L0_attn_x, L0_attn_qkv_w, L0_attn_out_w, L0_attn_hex_w, L0_attn_hamming_lambda_logit, L0_attn_q6_w, L0_attn_transforms, L0_attn_transform_weights, L0_attn_scale_logit, L0_attn_sips_alpha, L0_attn_sips_beta, L0_ffn_rw1, L0_ffn_rb1, L0_ffn_rw2, L0_ffn_rb2, L0_ffn_w1, L0_ffn_b1, L0_ffn_w2, L0_ffn_b2, L0_c, L0_wmod):

    def _L0_attn_ref(x, qkv_w, out_w, hex_w, hamming_lambda_logit, q6_w, transforms, transform_weights, scale_logit, sips_alpha, sips_beta):
        import jax, jax.numpy as jnp
        import numpy as np
        B, T, D, H, NT = (2, 512, 256, 16, 7)
        HD = D // H
        TEMP = 0.5
        b, t, _ = x.shape
        qkv = (x @ qkv_w.T).reshape(b, t, 3, H, HD)
        q = jnp.transpose(qkv[:, :, 0], (0, 2, 1, 3))
        k = jnp.transpose(qkv[:, :, 1], (0, 2, 1, 3))
        v = jnpp = jnp.transpose(qkv[:, :, 2], (0, 2, 1, 3))
        raw = jnp.einsum('bhid,bhjd->bhij', q, k)
        scores = sips_alpha[0] * jnp.tanh(raw / sips_beta[0])
        soft_bits = jnp.tanh(x @ hex_w.T)
        hamming = jnp.einsum('bid,bjd->bij', soft_bits, soft_bits) / 2.0
        lam = jax.nn.sigmoid(hamming_lambda_logit)
        scores = scores + lam * hamming[:, None, :, :]
        hexc = jnp.tanh(x @ q6_w.T)
        w = jax.nn.softmax(transform_weights / TEMP, axis=-1)
        Mh = jnp.einsum('ht,tde->hde', w, transforms)
        lat = jnp.einsum('bid,hde,bje->bhij', hexc, Mh, hexc) / 6.0
        lat = lat * (jax.nn.sigmoid(scale_logit) * 2.0)
        scores = scores + lat
        causal = jnp.tril(jnp.ones((t, t), bool))
        scores = jnp.where(causal[None, None], scores, -jnp.inf)
        attn = jax.nn.softmax(scores, axis=-1)
        out = jnp.einsum('bhij,bhjd->bhid', attn, v)
        out = jnp.transpose(out, (0, 2, 1, 3)).reshape(b, t, D)
        return out @ out_w.T

    def _L0_ffn_ref(x, rw1, rb1, rw2, rb2, w1, b1, w2, b2):
        import jax, jax.numpy as jnp
        import numpy as np
        EMB, HID, E, TOPK = (256, 1024, 8, 2)
        B, S, D = x.shape
        logits = jax.nn.silu(jnp.einsum('bsd,dh->bsh', x, rw1) + rb1)
        logits = jnp.einsum('bsh,he->bse', logits, rw2) + rb2
        k_logits, k_index = jax.lax.top_k(logits, TOPK)
        k_prob = jax.nn.softmax(k_logits, axis=-1)
        xf = x.reshape(B * S, D)
        k_index_f = k_index.reshape(B * S, TOPK)
        k_prob_f = k_prob.reshape(B * S, TOPK)
        out = jnp.zeros_like(xf)
        for e in range(E):
            we = jnp.sum(jnp.where(k_index_f == e, k_prob_f, 0.0), axis=-1)
            h = jax.nn.silu(xf @ w1[e] + b1[e]) @ w2[e] + b2[e]
            out = out + we[:, None] * h
        return out.reshape(B, S, D)
    x = L0_attn_x
    mod = (_silu(L0_c) @ L0_wmod).reshape(L0_c.shape[0], 6, 1, -1)
    sa, ca, ga, sb, cb, gb = (mod[:, 0], mod[:, 1], mod[:, 2], mod[:, 3], mod[:, 4], mod[:, 5])
    ga = (2 * (ga >= 0) - 1) * jnp.maximum(jnp.abs(ga), 0.25)
    gb = (2 * (gb >= 0) - 1) * jnp.maximum(jnp.abs(gb), 0.25)
    h = _layernorm(x, axis=-1) * (1 + ca) + sa
    x = x + ga * _L0_attn_ref(h, L0_attn_qkv_w, L0_attn_out_w, L0_attn_hex_w, L0_attn_hamming_lambda_logit, L0_attn_q6_w, L0_attn_transforms, L0_attn_transform_weights, L0_attn_scale_logit, L0_attn_sips_alpha, L0_attn_sips_beta)
    h = _layernorm(x, axis=-1) * (1 + cb) + sb
    x = x + gb * _L0_ffn_ref(h, L0_ffn_rw1, L0_ffn_rb1, L0_ffn_rw2, L0_ffn_rb2, L0_ffn_w1, L0_ffn_b1, L0_ffn_w2, L0_ffn_b2)
    return x

_drawn_inputs = setup_inputs


def setup_inputs(seed=0):
    import zlib

    import numpy as np

    out = dict(_drawn_inputs(seed))
    spreads = {'L0_ffn_rb1': (0.0, 0.648),
     'L0_ffn_rb2': (0.0, 0.373),
     'L0_ffn_b1': (0.0, 0.8),
     'L0_ffn_b2': (0.0, 0.455)}
    factors = {'L0_attn_qkv_w': 2.786,
     'L0_attn_out_w': 2.722,
     'L0_attn_hex_w': 8.0,
     'L0_attn_q6_w': 8.0,
     'L0_attn_transforms': 8.0,
     'L0_attn_transform_weights': 8.0,
     'L0_ffn_rw1': 2.934,
     'L0_ffn_rw2': 2.809,
     'L0_ffn_w1': 3.048,
     'L0_ffn_w2': 2.871}
    for name, (base, spread) in spreads.items():
        noise = np.random.default_rng([zlib.crc32(name.encode()), seed]).standard_normal(out[name].shape)
        drawn = base * np.exp(spread * noise) if base else spread * noise
        out[name] = jnp.asarray(drawn.astype(out[name].dtype))
    for name, factor in factors.items():
        out[name] = (out[name] * factor).astype(out[name].dtype)
    return out
```

```python
from contextlib import ExitStack

import concourse.bass as bass
from concourse import mybir

ACT = mybir.ActivationFunctionType
ALU = mybir.AluOpType
F32 = mybir.dt.float32
F32R = mybir.dt.float32r
U32 = mybir.dt.uint32
AX_X = mybir.AxisListType.X
ds = bass.ds

P = 128
B, T, D, H, HD, NT, HEX = 2, 2048, 256, 16, 16, 7, 6
NTOK = B * T
HID, E, TOPK = 1024, 8, 2
KC = D // P
BLK = 512
TPB = BLK // P
NBLK = T // BLK
NTILE = NTOK // P
HG = 4
NG = H // HG
NIT = B * NG
ROWS = 64
HROWS = 2 * HEX
BIAS_ROWS = 4 * HROWS + 2
VW = 32
SAFE = 60.0
EPS = 1e-5
NET = -(-(NTOK * TOPK // P + E) // 2) * 2
ROWS_E = NET * P
REGION = NTOK + P
VOID = E * REGION
LW = 32
N_RBLK = B * NBLK

STEPS = [(qb, kt) for qb in range(NBLK) for kt in range(TPB * (qb + 1))]
NSTEP = len(STEPS)
LAST_OF = {qb: max(s for s, (q, _) in enumerate(STEPS) if q == qb) for qb in range(NBLK)}
DIAG = [s for s, (qb, kt) in enumerate(STEPS) if kt >= TPB * qb]
PE_LEAD = 3
DVE_LEAD = 2
NBUF = 4
assert NSTEP % NBUF == 0


def query_offset(step):
    qb, kt = STEPS[step]
    return max(0, kt - TPB * qb) * P


def build(nc, a, out):
    dram = {}

    def scratch(name, shape, dt=F32):
        dram[name] = nc.dram_tensor(name, shape, dt, kind="Internal").ap()

    scratch("q_split", (B * H * ROWS, T))
    scratch("k_split", (B * H * ROWS, T))
    scratch("u_split", (B * H * ROWS, T))
    scratch("w_split", (NIT * ROWS, T))
    scratch("v_rows", (NIT * T, HG * VW))
    scratch("o_t", (NIT * P, T))
    scratch("x1", (NTOK, D))
    scratch("x_rows", (VOID + P, D))
    scratch("y_rows", (ROWS_E, D))

    with ExitStack() as ctx:
        modrow = ctx.enter_context(nc.sbuf_tensor("modrow", [P, B * 6 * D], F32))
        ident = ctx.enter_context(nc.sbuf_tensor("ident", [P, P], F32))
        scal = ctx.enter_context(nc.sbuf_tensor("scal", [P, 16], F32))
        with ExitStack() as c2:
            x_sb = c2.enter_context(nc.sbuf_tensor("x_sb", [P, NTILE * D], F32))
            stats = c2.enter_context(nc.sbuf_tensor("stats", [P, NTILE * 2], F32))
            rstd = c2.enter_context(nc.sbuf_tensor("rstd", [P, NTILE], F32))
            lattice = c2.enter_context(nc.sbuf_tensor("lattice", [HEX, H * HEX], F32))
            stage_modulation(nc, a, modrow, ident, scal, x_sb, stats, rstd, lattice)
            stage_projection(nc, a, dram, modrow, ident, scal, x_sb, lattice)
        stage_attention(nc, dram, scal)
        sb = lambda scope, n, shape, dt=F32: scope.enter_context(nc.sbuf_tensor(n, shape, dt))
        top_logit = sb(ctx, "top_logit", [P, NTILE * TOPK])
        top_index = sb(ctx, "top_index", [P, NTILE * TOPK])
        prob = sb(ctx, "prob", [P, NTILE * TOPK])
        slot_row = sb(ctx, "slot_row", [P, NTILE * TOPK], U32)
        tile_expert = sb(ctx, "tile_expert", [P, NET], U32)
        tile_row = sb(ctx, "tile_row", [P, NET], U32)
        zeros = sb(ctx, "zeros", [P, D])
        scattered = ctx.enter_context(nc.semaphore("scattered"))
        weights_in = ctx.enter_context(nc.semaphore("weights_in"))
        with ExitStack() as c2:
            h2_sb = sb(c2, "h2_sb", [P, NTILE * D])
            with ExitStack() as c3:
                x1_sb = sb(c3, "x1_sb", [P, NTILE * D])
                stats2 = sb(c3, "stats2", [P, NTILE * 2])
                rstd2 = sb(c3, "rstd2", [P, NTILE])
                stage_output(nc, a, dram, modrow, ident, x1_sb, stats2, rstd2, zeros)
                stage_router(nc, a, dram, modrow, ident, x1_sb, h2_sb, stats2, rstd2, top_logit, top_index,
                             scattered)
            with ExitStack() as c3:
                w1 = sb(c3, "w1", [P, E * KC * HID])
                w2 = sb(c3, "w2", [P, E * HID // P * D])
                b2 = sb(c3, "b2", [P, E * D])
                stage_dispatch(nc, a, dram, top_logit, top_index, prob, slot_row, tile_expert, tile_row,
                               zeros, scattered, w1, w2, b2, weights_in)
                assert NTILE * D == E * HID
                stage_experts(nc, a, dram, ident, tile_expert, tile_row, w1, w2, h2_sb, b2, weights_in)
        stage_combine(nc, a, dram, modrow, prob, slot_row, out)


HAM, SCALE, ALPHA, BETA, SIG_HAM, SIG_SCALE, HALF_LAM, LAT_SCALE, INV_BETA, ROOM = range(10)


def stage_modulation(nc, a, modrow, ident, scal, x_sb, stats, rstd, lattice):
    with ExitStack() as ctx:
        sb = lambda n, s, dt=F32: ctx.enter_context(nc.sbuf_tensor(n, s, dt))
        sem = lambda n: ctx.enter_context(nc.semaphore(n))
        wmod = sb("wmod", [P, KC, 6 * D])
        c_t = sb("c_t", [P, KC, B])
        c_silu = sb("c_silu", [P, KC, B])
        c_wide = sb("c_wide", [P, KC, B, P])
        bn = sb("bn", [P, NTILE, 6])
        gate = sb("gate", [P, D])
        gate_abs = sb("gate_abs", [P, D])
        gate_sign = sb("gate_sign", [P, D])
        trans = sb("trans", [HEX, NT, HEX])
        tw = sb("tw", [HEX, H, NT])
        tw_max = sb("tw_max", [HEX, H])
        tw_sum = sb("tw_sum", [HEX, H])
        lat_term = sb("lat_term", [HEX, H, HEX])
        mod_ps = ctx.enter_context(nc.psum_tensor("mod_ps", [P, B * 6 * D], F32))
        c_in, w_in, x_in, small_in = sem("c_in"), sem("w_in"), sem("x_in"), sem("small_in")
        silu_done, wide_done, mod_done = sem("silu_done"), sem("wide_done"), sem("mod_done")
        var_ready, std_ready, exp_in_ready, exp_ready = (
            sem("var_ready"), sem("std_ready"), sem("exp_in_ready"), sem("exp_ready"))
        chain = sem("mod_chain")
        block = ctx.enter_context(nc.Block())

        @block.sync
        def _(sp):
            sp.dma_start(c_t[:, :, :], a["c_t"].rearrange("(k p) b -> p k b", p=P)).then_inc(c_in, 16)
            sp.dma_start(wmod[:, :, :], a["wmod"].rearrange("(k p) n -> p k n", p=P)).then_inc(w_in, 16)
            sp.dma_start(ident[:, :], a["ident"]).then_inc(small_in, 16)
            sp.dma_start(scal[:, 0:4], a["scalars"].partition_broadcast(P)).then_inc(small_in, 16)
            sp.dma_start(trans[:, :, :], a["transforms"]).then_inc(small_in, 16)
            sp.dma_start(tw[:, :, :].rearrange("p h t -> p (h t)"),
                         a["transform_weights"].partition_broadcast(HEX)).then_inc(small_in, 16)
            sp.dma_start(x_sb[:, :].rearrange("p (n d) -> p n d", d=D),
                         a["x"].rearrange("(n p) d -> p n d", p=P)).then_inc(x_in, 16)

        @block.scalar
        def _(act):
            act.wait_ge(c_in, 16)
            act.activation(c_silu[:, :, :], c_t[:, :, :], ACT.Silu).then_inc(silu_done, 1)
            act.wait_ge(small_in, 64)
            act.activation(scal[:, SIG_HAM:SIG_SCALE + 1], scal[:, HAM:SCALE + 1], ACT.Exp,
                           scale=-1.0).then_inc(exp_ready, 1)
            act.wait_ge(exp_in_ready, 1)
            act.activation(tw[:, :, :], tw[:, :, :], ACT.Exp, scale=2.0).then_inc(exp_ready, 1)
            act.wait_ge(var_ready, 1)
            act.activation(rstd[:, :], rstd[:, :], ACT.Sqrt).then_inc(std_ready, 1)

        @block.tensor
        def _(pe):
            pe.wait_ge(w_in, 16)
            pe.wait_ge(wide_done, 1)
            for b in range(B):
                for n in range(3):
                    col = b * 6 * D + n * BLK
                    for k in range(KC):
                        mm = pe.matmul(mod_ps[:, col:col + BLK], c_wide[:, k, b, :],
                                       wmod[:, k, n * BLK:(n + 1) * BLK], start=(k == 0), stop=(k == KC - 1))
            mm.then_inc(mod_done, 1)

        @block.vector
        def _(dve):
            done = [0]

            def then_wait(ins):
                done[0] += 1
                ins.then_inc(chain, 1)
                dve.wait_ge(chain, done[0])

            dve.wait_ge(silu_done, 1)
            dve.tensor_copy(c_wide[:, :, :, :],
                            c_silu[:, :, :].rearrange("p k (b o) -> p k b o", o=1).broadcast_to([P, KC, B, P])
                            ).then_inc(wide_done, 1)
            dve.wait_ge(small_in, 64)
            then_wait(dve.tensor_reduce(tw_max[:, :], tw[:, :, :], AX_X, ALU.max))
            dve.tensor_tensor(tw[:, :, :], tw[:, :, :],
                              tw_max[:, :].rearrange("p (h o) -> p h o", o=1).broadcast_to([HEX, H, NT]),
                              ALU.subtract).then_inc(exp_in_ready, 1)
            dve.wait_ge(exp_ready, 2)
            then_wait(dve.tensor_scalar(scal[:, SIG_HAM:SIG_SCALE + 1], scal[:, SIG_HAM:SIG_SCALE + 1],
                                        1.0, None, ALU.add))
            then_wait(dve.reciprocal(scal[:, SIG_HAM:SIG_SCALE + 1], scal[:, SIG_HAM:SIG_SCALE + 1]))
            dve.tensor_scalar(scal[:, HALF_LAM:HALF_LAM + 1], scal[:, SIG_HAM:SIG_HAM + 1], 0.5, None, ALU.mult)
            dve.tensor_scalar(scal[:, LAT_SCALE:LAT_SCALE + 1], scal[:, SIG_SCALE:SIG_SCALE + 1],
                              2.0 / 6.0, None, ALU.mult)
            dve.reciprocal(scal[:, INV_BETA:INV_BETA + 1], scal[:, BETA:BETA + 1])
            then_wait(dve.scalar_tensor_tensor(scal[:, ROOM:ROOM + 1], scal[:, ALPHA:ALPHA + 1], -1.0,
                                               scal[:, ALPHA:ALPHA + 1], ALU.mult, ALU.min))
            then_wait(dve.tensor_scalar(scal[:, ROOM:ROOM + 1], scal[:, ROOM:ROOM + 1], SAFE, None, ALU.add))
            then_wait(dve.tensor_reduce(tw_sum[:, :], tw[:, :, :], AX_X, ALU.add))
            then_wait(dve.reciprocal(tw_sum[:, :], tw_sum[:, :]))
            then_wait(dve.tensor_scalar(tw_sum[:, :], tw_sum[:, :], scal[0:HEX, LAT_SCALE:LAT_SCALE + 1], None,
                                        ALU.mult))
            then_wait(dve.tensor_tensor(tw[:, :, :], tw[:, :, :],
                                        tw_sum[:, :].rearrange("p (h o) -> p h o", o=1).broadcast_to([HEX, H, NT]),
                                        ALU.mult))
            lat3 = lattice[:, :].rearrange("p (h e) -> p h e", e=HEX)
            for t in range(NT):
                dst = lat3 if t == 0 else lat_term[:, :, :]
                then_wait(dve.tensor_tensor(dst, trans[:, t:t + 1, :].broadcast_to([HEX, H, HEX]),
                                            tw[:, :, t:t + 1].broadcast_to([HEX, H, HEX]), ALU.mult))
                if t:
                    then_wait(dve.tensor_tensor(lat3, lat3, lat_term[:, :, :], ALU.add))
            dve.wait_ge(x_in, 16)
            for n in range(NTILE):
                last = dve.bn_stats(bn[:, n, :], x_sb[:, n * D:(n + 1) * D])
            then_wait(last)
            for n in range(NTILE):
                last = dve.bn_aggr(stats[:, 2 * n:2 * n + 2], bn[:, n, :])
            then_wait(last)
            dve.tensor_scalar(rstd[:, :], stats[:, :].rearrange("p (n s) -> p n s", s=2)[:, :, 1], EPS, None,
                              ALU.add).then_inc(var_ready, 1)
            dve.wait_ge(std_ready, 1)
            then_wait(dve.reciprocal(rstd[:, :], rstd[:, :]))
            for n in range(NTILE):
                tile = x_sb[:, n * D:(n + 1) * D]
                dve.tensor_scalar(tile, tile, stats[:, 2 * n:2 * n + 1], rstd[:, n:n + 1], ALU.subtract, ALU.mult)
            dve.wait_ge(mod_done, 1)
            for b in range(B):
                for part in range(6):
                    cols = slice((b * 6 + part) * D, (b * 6 + part + 1) * D)
                    if part % 3 == 0:
                        dve.tensor_copy(modrow[:, cols], mod_ps[:, cols])
                    elif part % 3 == 1:
                        dve.tensor_scalar(modrow[:, cols], mod_ps[:, cols], 1.0, None, ALU.add)
                    else:
                        then_wait(dve.tensor_copy(gate[:, :], mod_ps[:, cols]))
                        then_wait(dve.scalar_tensor_tensor(gate_abs[:, :], gate[:, :], -1.0, gate[:, :],
                                                           ALU.mult, ALU.max))
                        then_wait(dve.tensor_scalar(gate_abs[:, :], gate_abs[:, :], 0.25, None, ALU.max))
                        then_wait(dve.tensor_scalar(gate_sign[:, :], mod_ps[:, cols], 0.0, 2.0,
                                                    ALU.is_ge, ALU.mult))
                        then_wait(dve.scalar_tensor_tensor(modrow[:, cols], gate_sign[:, :], -1.0,
                                                           gate_abs[:, :], ALU.add, ALU.mult))


def stage_projection(nc, a, dram, modrow, ident, scal, x_sb, lattice):
    with ExitStack() as ctx:
        sb = lambda n, s, dt=F32: ctx.enter_context(nc.sbuf_tensor(n, s, dt))
        ps = lambda n, s: ctx.enter_context(nc.psum_tensor(n, s, F32))
        sem = lambda n: ctx.enter_context(nc.semaphore(n))
        wqkv = sb("wqkv", [P, KC, 3 * D])
        wcode = sb("wcode", [P, KC, HROWS])
        head_sum = sb("head_sum", [H * HEX, H])
        soft_sum = sb("soft_sum", [HROWS, H])
        xm = sb("xm", [P, D])
        h = sb("h", [P, 2, D])
        h_t = sb("h_t", [P, KC, BLK])
        qk_hi = sb("qk_hi", [P, 4, BLK], F32R)
        qk_lo = sb("qk_lo", [P, 4, BLK], F32R)
        code = sb("code", [HROWS, BLK])
        w_hi = sb("w_hi", [HROWS, BLK], F32R)
        w_lo = sb("w_lo", [HROWS, BLK], F32R)
        soft = sb("soft", [HROWS, BLK])
        s_hi = sb("s_hi", [HROWS, BLK], F32R)
        s_lo = sb("s_lo", [HROWS, BLK], F32R)
        soft_abs = sb("soft_abs", [HROWS, BLK])
        l_hi = sb("l_hi", [H * HEX, BLK], F32R)
        l_lo = sb("l_lo", [H * HEX, BLK], F32R)
        lat_abs = sb("lat_abs", [H * HEX, BLK])
        guard = sb("guard", [H, BLK])
        g_hi = sb("g_hi", [H, BLK], F32R)
        g_lo = sb("g_lo", [H, BLK], F32R)
        v_st = sb("v_st", [P, TPB, H, VW])
        tv_ps = ps("tv_ps", [P, 2 * BLK])
        qk_ps = ps("qk_ps", [P, 4 * BLK])
        code_ps = ps("code_ps", [P, BLK])
        lat_ps = ps("lat_ps", [P, BLK])

        w_in, waited = sem("pw_in"), sem("p_waited")
        norm_step, h_ready, transposed, h_t_ready = (
            sem("norm_step"), sem("h_ready"), sem("transposed"), sem("h_t_ready"))
        code_mm, qk_mm, lat_mm, v_mm, guard_mm = (
            sem("code_mm"), sem("qk_mm"), sem("lat_mm"), sem("v_mm"), sem("guard_mm"))
        code_ready, hi_ready, lo_ready, v_ready, lat_act, soft_ready, soft_abs_ready = (
            sem("code_ready"), sem("hi_ready"), sem("lo_ready"), sem("v_ready"), sem("lat_act"),
            sem("soft_ready"), sem("soft_abs_ready"))
        w_ready, s_ready, lat_ready, guard_step, g_ready = (
            sem("w_ready"), sem("s_ready"), sem("lat_ready"), sem("guard_step"), sem("g_ready"))
        st_qk = [sem(f"st_qk{m}") for m in range(4)]
        st_w, st_s, st_l, st_g, st_v = sem("st_w"), sem("st_s"), sem("st_l"), sem("st_g"), sem("st_v")
        block = ctx.enter_context(nc.Block())

        N_QK, N_W, N_S, N_L, N_G, N_V = 4, 4 * NG, 4, 4, 2, TPB
        ST_0, TRANS_0, LO_0, LAT_0, V_0, GUARD_0, GMM_0, SABS_0, H_0 = 16, 2, 4, 1, 1, 2, 1, 1, 1

        def split_rows(name, r0, count, b, c):
            view = dram[name].rearrange("(z h r) t -> z h r t", h=H, r=ROWS)
            return view[ds(b, 1), :, r0:r0 + count, ds(c * BLK, BLK)].rearrange("z h r t -> (z h) r t")

        @block.sync
        def _(sp):
            for s in st_qk + [st_w, st_s, st_l, st_g, st_v]:
                sp.sem_inc(s, ST_0)
            sp.dma_start(wcode[:, :, :], a["code_wt"].rearrange("(k p) n -> p k n", p=P)).then_inc(w_in, 16)
            sp.dma_start(wqkv[:, :, :], a["qkv_wt"].rearrange("(k p) n -> p k n", p=P)).then_inc(w_in, 16)
            sp.dma_start(head_sum[:, :], a["head_sum"]).then_inc(w_in, 16)
            sp.dma_start(soft_sum[:, :], a["soft_sum"]).then_inc(w_in, 16)
            with sp.Fori(0, B) as b, sp.Fori(0, NBLK) as c:
                i = b * NBLK + c
                cols = ds(c * BLK, BLK)
                sp.wait_ge(w_ready, i * 2 + 2)
                wv = dram["w_split"].rearrange("(z g r) t -> z g r t", g=NG, r=ROWS)
                for part in range(4):
                    for g in range(NG):
                        dst = wv[ds(b, 1), g, part * HROWS:(part + 1) * HROWS, cols]
                        sp.dma_start(dst.rearrange("z r t -> (z r) t"),
                                     (w_hi, w_lo)[part % 2][:, :].bitcast(F32)).then_inc(st_w, 16)
                sp.wait_ge(s_ready, i * 2 + 2)
                for part in range(4):
                    dst = split_rows("u_split", part * HROWS + HEX, HEX, b, c).rearrange("h r t -> r h t")
                    src = (s_hi, s_lo)[part // 2][HEX:HROWS, :].bitcast(F32)
                    sp.dma_start(dst, src.rearrange("r (o t) -> r o t", o=1).broadcast_to([HEX, H, BLK])
                                 ).then_inc(st_s, 16)
                for m in range(4):
                    sp.wait_ge(lo_ready, i * 4 + (LO_0 + m + 1))
                    sp.sem_inc(waited, 1)
                    for part in range(4):
                        hi_part = part // 2 == 0 if m < 2 else part % 2 == 0
                        dst = split_rows("q_split" if m < 2 else "k_split", part * HD, HD, b, c)
                        sp.dma_start(dst[(m % 2) * 8:(m % 2) * 8 + 8],
                                     (qk_hi if hi_part else qk_lo)[:, m, :].bitcast(F32)).then_inc(st_qk[m], 16)
                sp.wait_ge(lat_ready, i + (LAT_0 + 1))
                for part in range(4):
                    sp.dma_start(split_rows("u_split", part * HROWS, HEX, b, c),
                                 (l_hi, l_lo)[part // 2][:, :].bitcast(F32)).then_inc(st_l, 16)
                sp.wait_ge(v_ready, i + (V_0 + 1))
                vv = dram["v_rows"].rearrange("(z g n p) v -> z n p g v", z=B, g=NG, p=P)
                for t in range(TPB):
                    dst = vv[ds(b, 1), ds(c * TPB + t, 1)].rearrange("z n p g v -> (z n p) g v")
                    sp.dma_start(dst, v_st[:, t, :, :].rearrange("p (g h) v -> p g (h v)", g=NG)
                                 ).then_inc(st_v, 16)
                sp.wait_ge(g_ready, i + 1)
                for part, src in enumerate((g_hi, g_lo)):
                    dst = split_rows("u_split", 4 * HROWS + part, 1, b, c).rearrange("h r t -> (h r) t")
                    sp.dma_start(dst, src[:, :].bitcast(F32)).then_inc(st_g, 16)
            for s, n in [(s, N_QK) for s in st_qk] + [
                    (st_w, N_W), (st_s, N_S), (st_l, N_L), (st_g, N_G), (st_v, N_V)]:
                sp.wait_ge(s, ST_0 + 16 * n * B * NBLK)

        @block.gpsimd
        def _(pool):
            pool.sem_inc(h_ready, H_0)
            with pool.Fori(0, B) as b, pool.Fori(0, NBLK) as c:
                for t in range(TPB):
                    tile = b * (NBLK * TPB) + c * TPB + t
                    pool.wait_ge(h_ready, tile + H_0)
                    pool.sem_inc(waited, 1)
                    pool.tensor_tensor(xm[:, :], x_sb[:, ds(tile * D, D)], modrow[:, ds(b * (6 * D) + D, D)],
                                       ALU.mult).then_inc(norm_step, 1)
                    pool.wait_ge(norm_step, tile + 1)
                    pool.wait_ge(transposed, tile + (TRANS_0 - 1))
                    pool.sem_inc(waited, 1)
                    pool.tensor_tensor(h[:, t % 2, :], xm[:, :], modrow[:, ds(b * (6 * D), D)],
                                       ALU.add).then_inc(h_ready, 1)

        @block.tensor
        def _(pe):
            pe.sem_inc(transposed, TRANS_0)
            pe.sem_inc(guard_mm, GMM_0)
            pe.wait_ge(w_in, 64)
            with pe.Fori(0, B * NBLK) as i:
                pe.wait_ge(v_ready, i + V_0)
                for t in range(TPB):
                    pe.wait_ge(h_ready, i * TPB + (t + 1 + H_0))
                    for k in range(KC):
                        tr = pe.transpose(tv_ps[:, k * BLK + t * P:k * BLK + (t + 1) * P],
                                          h[:, t % 2, k * P:(k + 1) * P], ident[:, :])
                    tr.then_inc(transposed, 1)
                pe.wait_ge(h_t_ready, i + 1)
                pe.wait_ge(guard_step, i * 2 + (GUARD_0 - 1))
                for k in range(KC):
                    mm = pe.matmul(code_ps[0:HROWS, :], wcode[:, k, :], h_t[:, k, :],
                                   start=(k == 0), stop=(k == KC - 1))
                mm.then_inc(code_mm, 1)
                for m in range(4):
                    pe.wait_ge(lo_ready, i * 4 + (m + 1))
                    for k in range(KC):
                        mm = pe.matmul(qk_ps[:, m * BLK:(m + 1) * BLK], wqkv[:, k, m * P:(m + 1) * P],
                                       h_t[:, k, :], start=(k == 0), stop=(k == KC - 1))
                    mm.then_inc(qk_mm, 1)
                pe.wait_ge(code_ready, i + 1)
                pe.wait_ge(lat_ready, i + LAT_0)
                pe.matmul(lat_ps[0:H * HEX, :], lattice[:, :], code[0:HEX, :],
                          start=True, stop=True).then_inc(lat_mm, 1)
                for t in range(TPB):
                    for k in range(KC):
                        mm = pe.matmul(tv_ps[:, t * D:(t + 1) * D], h_t[:, k, t * P:(t + 1) * P],
                                       wqkv[:, k, 2 * D:3 * D], start=(k == 0), stop=(k == KC - 1))
                mm.then_inc(v_mm, 1)
                pe.wait_ge(lat_act, i + 1)
                pe.wait_ge(soft_abs_ready, i + (SABS_0 + 1))
                pe.matmul(code_ps[0:H, :], head_sum[:, :], lat_abs[:, :], start=True, stop=False)
                pe.matmul(code_ps[0:H, :], soft_sum[:, :], soft_abs[:, :], start=False, stop=True
                          ).then_inc(guard_mm, 1)

        @block.scalar
        def _(act):
            act.sem_inc(soft_abs_ready, SABS_0)
            with act.Fori(0, B * NBLK) as i:
                act.wait_ge(transposed, i * TPB + (TRANS_0 + TPB))
                act.activation(h_t[:, :, :], tv_ps[:, :].rearrange("p (k t) -> p k t", k=KC),
                               ACT.Copy).then_inc(h_t_ready, 1)
                act.wait_ge(code_mm, i + 1)
                act.activation(code[:, :], code_ps[0:HROWS, :], ACT.Tanh).then_inc(code_ready, 1)
                for m in range(4):
                    act.wait_ge(qk_mm, i * 4 + (m + 1))
                    act.wait_ge(st_qk[m], i * (16 * N_QK) + ST_0)
                    act.activation(qk_hi[:, m, :], qk_ps[:, m * BLK:(m + 1) * BLK], ACT.Copy,
                                   scale=scal[:, INV_BETA:INV_BETA + 1] if m < 2 else 1.0
                                   ).then_inc(hi_ready, 1)
                act.wait_ge(soft_ready, i + 1)
                act.wait_ge(guard_mm, i + GMM_0)
                act.activation(soft_abs[:, :], soft[:, :], ACT.Abs).then_inc(soft_abs_ready, 1)
                act.wait_ge(lat_mm, i + 1)
                act.activation(lat_abs[:, :], lat_ps[0:H * HEX, :], ACT.Abs)
                act.wait_ge(st_l, i * (16 * N_L) + ST_0)
                act.activation(l_hi[:, :], lat_ps[0:H * HEX, :], ACT.Copy).then_inc(lat_act, 1)

        @block.vector
        def _(dve):
            dve.sem_inc(lo_ready, LO_0)
            dve.sem_inc(lat_ready, LAT_0)
            dve.sem_inc(guard_step, GUARD_0)
            dve.memset(v_st[:, :, :, HD:VW], 1.0).then_inc(v_ready, V_0)
            with dve.Fori(0, B * NBLK) as i:
                dve.wait_ge(code_ready, i + 1)
                dve.wait_ge(st_w, i * (16 * N_W) + ST_0)
                dve.tensor_copy(w_hi[:, :], code[:, :]).then_inc(w_ready, 1)
                dve.wait_ge(soft_abs_ready, i + SABS_0)
                dve.tensor_scalar(soft[:, :], code[:, :], scal[0:HROWS, HALF_LAM:HALF_LAM + 1], None,
                                  ALU.mult).then_inc(soft_ready, 1)
                dve.wait_ge(w_ready, i * 2 + 1)
                dve.tensor_tensor(w_lo[:, :], code[:, :], w_hi[:, :].bitcast(F32), ALU.subtract
                                  ).then_inc(w_ready, 1)
                dve.wait_ge(soft_ready, i + 1)
                dve.wait_ge(st_s, i * (16 * N_S) + ST_0)
                dve.tensor_copy(s_hi[:, :], soft[:, :]).then_inc(s_ready, 1)
                dve.wait_ge(s_ready, i * 2 + 1)
                dve.tensor_tensor(s_lo[:, :], soft[:, :], s_hi[:, :].bitcast(F32), ALU.subtract
                                  ).then_inc(s_ready, 1)
                for m in range(4):
                    dve.wait_ge(hi_ready, i * 4 + (m + 1))
                    dve.scalar_tensor_tensor(qk_lo[:, m, :], qk_ps[:, m * BLK:(m + 1) * BLK],
                                             scal[:, INV_BETA:INV_BETA + 1] if m < 2 else 1.0,
                                             qk_hi[:, m, :].bitcast(F32), ALU.mult, ALU.subtract
                                             ).then_inc(lo_ready, 1)
                dve.wait_ge(lat_act, i + 1)
                dve.tensor_tensor(l_lo[:, :], lat_ps[0:H * HEX, :], l_hi[:, :].bitcast(F32), ALU.subtract
                                  ).then_inc(lat_ready, 1)
                dve.wait_ge(v_mm, i + 1)
                dve.wait_ge(st_v, i * (16 * N_V) + ST_0)
                dve.tensor_copy(v_st[:, :, :, 0:HD],
                                tv_ps[:, :].rearrange("p (t h d) -> p t h d", t=TPB, h=H)).then_inc(v_ready, 1)
                dve.wait_ge(guard_mm, i + (GMM_0 + 1))
                dve.tensor_scalar(guard[:, :], code_ps[0:H, :], -1.0, scal[0:H, ROOM:ROOM + 1],
                                  ALU.mult, ALU.add).then_inc(guard_step, 1)
                dve.wait_ge(guard_step, i * 2 + (GUARD_0 + 1))
                dve.wait_ge(st_g, i * (16 * N_G) + ST_0)
                dve.tensor_scalar(g_hi[:, :], guard[:, :], 0.0, None, ALU.min).then_inc(guard_step, 1)
                dve.wait_ge(guard_step, i * 2 + (GUARD_0 + 2))
                dve.scalar_tensor_tensor(g_lo[:, :], guard[:, :], 0.0, g_hi[:, :].bitcast(F32),
                                         ALU.min, ALU.subtract).then_inc(g_ready, 1)


def stage_attention(nc, dram, scal):
    with ExitStack() as ctx:
        sb = lambda n, s, dt=F32: ctx.enter_context(nc.sbuf_tensor(n, s, dt))
        ps = lambda n, s: ctx.enter_context(nc.psum_tensor(n, s, F32))
        sem = lambda n: ctx.enter_context(nc.semaphore(n))
        k_st = sb("k_st", [P, HG // 2, T], F32R)
        q_mv = sb("q_mv", [P, HG, T], F32R)
        w_st = sb("w_st", [P, T], F32R)
        u_mv = sb("u_mv", [P, HG, T], F32R)
        v_sb = sb("v_sb", [P, T // P, HG * VW])
        probs = sb("probs", [P, NBUF, HG, BLK])
        o_sb = sb("o_sb", [P, 2, BLK])
        raw_ps = ps("raw_ps", [P, HG, BLK])
        bil_ps = ps("bil_ps", [P, 2, BLK])
        o_ps = ps("o_ps", [P, BLK])
        pad_ready, waited = sem("pad_ready"), sem("a_waited")
        loaded = [sem(f"loaded{c}") for c in range(NBLK)]
        raw_mm, bil_mm, pv_mm = sem("raw_mm"), sem("bil_mm"), sem("pv_mm")
        tanh_ready, sum_ready, exp_ready, mask_ready = (
            sem("tanh_ready"), sem("sum_ready"), sem("exp_ready2"), sem("mask_ready"))
        o_ready = sem("o_ready")
        o_stored = [sem(f"o_stored{p}") for p in range(2)]
        block = ctx.enter_context(nc.Block())

        N_LOADS = 1 + 2 + 2 + 1
        PV_0, TANH_0, SUM_0, O_0, ST_0 = NSTEP, 1, 2, 1, 16

        def load_block(sp, it, c):
            cols = slice(c * BLK, (c + 1) * BLK)
            rows = lambda name: dram[name][ds(it * (HG * ROWS), HG * ROWS), cols]
            sp.wait_ge(pv_mm, it * NSTEP + (PV_0 - NSTEP + LAST_OF[NBLK - 1] - NBLK * TPB + 1 + (c + 1) * TPB))
            sp.dma_start(k_st[:, :, cols].bitcast(F32),
                         rows("k_split").rearrange("(j p) t -> p j t", p=P)).then_inc(loaded[c], 16)
            q_rows = rows("q_split").rearrange("(j z r) t -> z r j t", z=2, r=ROWS)
            for z in range(2):
                sp.dma_start(q_mv[z * ROWS:(z + 1) * ROWS, z::2, cols].bitcast(F32), q_rows[z]
                             ).then_inc(loaded[c], 16)
            u_rows = rows("u_split").rearrange("(j r) t -> r j t", r=ROWS)
            sp.dma_start(u_mv[0:BIAS_ROWS, :, cols].bitcast(F32), u_rows[0:BIAS_ROWS]).then_inc(loaded[c], 16)
            sp.dma_start(w_st[0:4 * HROWS, cols].bitcast(F32),
                         dram["w_split"][ds(it * ROWS, 4 * HROWS), cols]).then_inc(loaded[c], 16)
            sp.dma_start(v_sb[:, c * TPB:(c + 1) * TPB, :],
                         dram["v_rows"][ds(it * T + c * BLK, BLK), :].rearrange("(n p) v -> p n v", p=P)
                         ).then_inc(loaded[c], 16)

        def store_out(sp, it, qb):
            sp.wait_ge(o_ready, it * NBLK + (O_0 + qb + 1))
            sp.dma_start(dram["o_t"][ds(it * P, P), qb * BLK:(qb + 1) * BLK],
                         o_sb[:, qb % 2, :]).then_inc(o_stored[qb % 2], 16)

        @block.sync
        def _(sp):
            for s in o_stored:
                sp.sem_inc(s, ST_0)
            sp.wait_ge(pad_ready, 4)
            for c in range(NBLK):
                load_block(sp, 0, c)

            def iteration(it, last):
                for qb in range(NBLK):
                    if qb == NBLK - 1 and not last:
                        for c in range(NBLK):
                            load_block(sp, it + 1, c)
                    store_out(sp, it, qb)

            with sp.Fori(0, NIT - 1) as it:
                iteration(it, False)
            iteration(NIT - 1, True)
            for s in o_stored:
                sp.wait_ge(s, ST_0 + 16 * NIT * NBLK // 2)

        @block.gpsimd
        def _(pool):
            pool.memset(q_mv[:, :, :].bitcast(U32), 0).then_inc(pad_ready, 1)
            pool.memset(u_mv[:, :, :].bitcast(U32), 0).then_inc(pad_ready, 1)
            with pool.Fori(0, NIT) as it:
                for s in DIAG:
                    first = query_offset(s)
                    pool.wait_ge(exp_ready, it * NSTEP + (s + 1))
                    pool.sem_inc(waited, 1)
                    tri = probs[:, s % NBUF, :, first:first + P]
                    pool.affine_select(out=tri, in_=tri, compare_op=ALU.is_ge, fill=0.0, base=0,
                                       pattern=[[0, HG], [1, P]], channel_multiplier=-1).then_inc(mask_ready, 1)

        @block.tensor
        def _(pe):
            pe.sem_inc(pv_mm, PV_0)

            def raw_scores(it, s):
                qb, kt = STEPS[s]
                first = query_offset(s)
                if kt == 0:
                    pe.wait_ge(loaded[qb], it * (16 * N_LOADS) + 16 * N_LOADS)
                pe.wait_ge(tanh_ready, it * NSTEP + (s + TANH_0))
                for hd in range(HG):
                    mm = pe.matmul(raw_ps[:, hd, first:BLK], k_st[:, hd // 2, kt * P:(kt + 1) * P],
                                   q_mv[:, hd, qb * BLK + first:(qb + 1) * BLK], start=True, stop=True)
                mm.then_inc(raw_mm, 1)

            def bilinear(it, s, heads):
                qb, kt = STEPS[s]
                first = query_offset(s)
                for hd in heads:
                    pe.wait_ge(sum_ready, it * (HG * NSTEP) + (HG * s + hd - 1 + SUM_0))
                    pe.matmul(bil_ps[:, hd % 2, first:BLK], w_st[:, kt * P:(kt + 1) * P],
                              u_mv[:, hd, qb * BLK + first:(qb + 1) * BLK], start=True, stop=True
                              ).then_inc(bil_mm, 1)

            def weighted_values(it, s):
                qb, kt = STEPS[s]
                first = query_offset(s)
                if s in DIAG:
                    pe.wait_ge(mask_ready, it * len(DIAG) + (DIAG.index(s) + 1))
                else:
                    pe.wait_ge(exp_ready, it * NSTEP + (s + 1))
                if kt == 0:
                    pe.wait_ge(o_ready, it * NBLK + (qb + O_0))
                for hd in range(HG):
                    mm = pe.matmul(o_ps[hd * VW:(hd + 1) * VW, first:BLK],
                                   v_sb[:, kt, hd * VW:(hd + 1) * VW], probs[:, s % NBUF, hd, first:BLK],
                                   start=(kt == 0), stop=(s == LAST_OF[qb]))
                mm.then_inc(pv_mm, 1)

            FIRST_TWO, LAST_TWO = (0, 1), (2, 3)
            for s in range(PE_LEAD):
                raw_scores(0, s)
                if s:
                    bilinear(0, s - 1, LAST_TWO)
                bilinear(0, s, FIRST_TWO)

            def iteration(it, last):
                for s in range(NSTEP):
                    at = lambda n: (it, n) if n < NSTEP else None if last else (it + 1, n - NSTEP)
                    if at(s + PE_LEAD):
                        raw_scores(*at(s + PE_LEAD))
                    if at(s + PE_LEAD - 1):
                        bilinear(*at(s + PE_LEAD - 1), LAST_TWO)
                    weighted_values(it, s)
                    if at(s + PE_LEAD):
                        bilinear(*at(s + PE_LEAD), FIRST_TWO)

            with pe.Fori(0, NIT - 1) as it:
                iteration(it, False)
            iteration(NIT - 1, True)

        @block.scalar
        def _(act):
            act.sem_inc(tanh_ready, TANH_0)

            def tanh(it, s):
                first = query_offset(s)
                act.wait_ge(raw_mm, it * NSTEP + (s + 1))
                act.wait_ge(pv_mm, it * NSTEP + (PV_0 + s + 1 - NBUF))
                act.activation(probs[:, s % NBUF, :, first:BLK], raw_ps[:, :, first:BLK], ACT.Tanh
                               ).then_inc(tanh_ready, 1)

            def exp(it, s):
                first = query_offset(s)
                act.wait_ge(sum_ready, it * (HG * NSTEP) + (HG * (s + 1) + SUM_0))
                scores = probs[:, s % NBUF, :, first:BLK]
                act.activation(scores, scores, ACT.Exp).then_inc(exp_ready, 1)

            tanh(0, 0)

            def iteration(it, last):
                for s in range(NSTEP):
                    if s + 1 < NSTEP:
                        tanh(it, s + 1)
                    elif not last:
                        tanh(it + 1, 0)
                    exp(it, s)

            with act.Fori(0, NIT - 1) as it:
                iteration(it, False)
            iteration(NIT - 1, True)

        @block.vector
        def _(dve):
            dve.memset(w_st[0:ROWS, :].bitcast(F32), 1.0).then_inc(pad_ready, 1)
            dve.memset(w_st[ROWS:P, :].bitcast(F32), 0.0).then_inc(pad_ready, 1)
            dve.sem_inc(sum_ready, SUM_0)
            dve.sem_inc(o_ready, O_0)

            def score_sums(it, s):
                first = query_offset(s)
                dve.wait_ge(tanh_ready, it * NSTEP + (s + 1 + TANH_0))
                for hd in range(HG):
                    dve.wait_ge(bil_mm, it * (HG * NSTEP) + (HG * s + hd + 1))
                    scores = probs[:, s % NBUF, hd, first:BLK]
                    dve.scalar_tensor_tensor(scores, scores, scal[:, ALPHA:ALPHA + 1],
                                             bil_ps[:, hd % 2, first:BLK], ALU.mult, ALU.add
                                             ).then_inc(sum_ready, 1)

            def evacuate(it, qb):
                dve.wait_ge(pv_mm, it * NSTEP + (PV_0 + LAST_OF[qb] + 1))
                dve.wait_ge(o_stored[qb % 2], it * (16 * NBLK // 2) + (16 * (qb // 2) + ST_0))
                dve.tensor_copy(o_sb[:, qb % 2, :], o_ps[:, :]).then_inc(o_ready, 1)

            for s in range(DVE_LEAD):
                score_sums(0, s)

            def iteration(it, last):
                for s in range(NSTEP):
                    ahead = s + DVE_LEAD
                    if ahead < NSTEP:
                        score_sums(it, ahead)
                    elif not last:
                        score_sums(it + 1, ahead - NSTEP)
                    if s == LAST_OF[STEPS[s][0]]:
                        evacuate(it, STEPS[s][0])

            with dve.Fori(0, NIT - 1) as it:
                iteration(it, False)
            iteration(NIT - 1, True)


def skewed(eng, total, lag, unroll, emit):
    peeled = -(-lag // unroll) * unroll
    for m in range(peeled):
        emit(m, m, lambda k: 0 <= m - k < total)
    with eng.Fori(peeled // unroll, total // unroll) as i:
        for u in range(unroll):
            emit(i * unroll + u, u, lambda k: True)
    for m in range(total, total + lag):
        emit(m, m, lambda k: 0 <= m - k < total)


def stage_output(nc, a, dram, modrow, ident, x1_sb, stats2, rstd2, zeros):
    with ExitStack() as ctx:
        sb = lambda n, s, dt=F32: ctx.enter_context(nc.sbuf_tensor(n, s, dt))
        ps = lambda n, s: ctx.enter_context(nc.psum_tensor(n, s, F32))
        sem = lambda n: ctx.enter_context(nc.semaphore(n))
        OB = 4
        wo = sb("wo", [P, KC, D])
        o_t = sb("o_t_sb", [P, OB, NG, P])
        rden = sb("rden", [P, H])
        attn = sb("attn", [P, 2, D])
        attn_t = sb("attn_t", [P, 2, D])
        gated = sb("gated", [P, D])
        bn = sb("bn2", [P, NTILE * 6])
        o_tr_ps = ps("o_tr_ps", [P, 2, BLK])
        a_tr_ps = ps("a_tr_ps", [P, 2, BLK])
        proj_ps = ps("proj_ps", [P, 2, BLK])
        waited = sem("o_waited")
        w_in, x_in, zero_ready, zero_stored = sem("wo_in"), sem("x1_in"), sem("zero_ready"), sem("zero_stored")
        o_in = [sem(f"o_in{p}") for p in range(OB)]
        o_tr_mm, a_tr_mm, proj_mm = sem("o_tr_mm"), sem("a_tr_mm"), sem("proj_mm")
        rden_ready, attn_ready, attn_t_ready, gated_ready, x1_ready, stats_ready, var_ready, std_ready = (
            sem("rden_ready"), sem("attn_ready"), sem("attn_t_ready"), sem("gated_ready"), sem("x1_ready"),
            sem("stats_ready"), sem("var_ready2"), sem("std_ready2"))
        block = ctx.enter_context(nc.Block())
        OTR_0, ATTN_0, ATR_0, ATT_0, PROJ_0, GATED_0, X1_0 = OB, 2, 2, 2, 2, 2, 1

        @block.sync
        def _(sp):
            ov = dram["o_t"].rearrange("(z g p) t -> z p g t", g=NG, p=P)

            def load(m, u, active):
                if active(0):
                    sp.wait_ge(o_tr_mm, m + (OTR_0 - OB + 1))
                    sp.sem_inc(waited, 1)
                    src = ov[ds(m // (NBLK * TPB), 1), :, :, ds(m % (NBLK * TPB) * P, P)]
                    sp.dma_start(o_t[:, u % OB, :, :], src.rearrange("z p g t -> (z p) g t")
                                 ).then_inc(o_in[u % OB], 16)

            sp.dma_start(wo[:, :, :], a["out_wt"].rearrange("(k p) n -> p k n", p=P)).then_inc(w_in, 16)
            sp.dma_start(x1_sb[:, :].rearrange("p (n d) -> p n d", d=D),
                         a["x"].rearrange("(n p) d -> p n d", p=P)).then_inc(x_in, 16)
            skewed(sp, NTILE, 0, OB, load)
            sp.wait_ge(zero_ready, 1)
            sp.dma_start(dram["x_rows"][VOID:VOID + P, :], zeros[:, :]).then_inc(zero_stored, 16)
            sp.wait_ge(zero_stored, 16)

        @block.tensor
        def _(pe):
            pe.sem_inc(o_tr_mm, OTR_0)
            pe.sem_inc(proj_mm, PROJ_0)
            pe.sem_inc(a_tr_mm, ATR_0)
            pe.wait_ge(w_in, 16)

            def step(m, u, active):
                if active(0):
                    pe.wait_ge(o_in[u % OB], (m // OB) * 16 + 16)
                    pe.wait_ge(attn_ready, m + (ATTN_0 - 1))
                    for g in range(NG):
                        tr = pe.transpose(o_tr_ps[:, u % 2, g * P:(g + 1) * P], o_t[:, u % OB, g, :], ident[:, :])
                    tr.then_inc(o_tr_mm, 1)
                if active(1):
                    n, p = m - 1, (u - 1) % 2
                    pe.wait_ge(attn_ready, n + (ATTN_0 + 1))
                    pe.wait_ge(attn_t_ready, n + (ATT_0 - 1))
                    for k in range(KC):
                        tr = pe.transpose(a_tr_ps[:, p, k * P:(k + 1) * P], attn[:, p, k * P:(k + 1) * P],
                                          ident[:, :])
                    tr.then_inc(a_tr_mm, 1)
                if active(2):
                    n, p = m - 2, u % 2
                    pe.wait_ge(attn_t_ready, n + (ATT_0 + 1))
                    pe.wait_ge(gated_ready, n + (GATED_0 - 1))
                    for k in range(KC):
                        mm = pe.matmul(proj_ps[:, p, 0:D], attn_t[:, p, k * P:(k + 1) * P], wo[:, k, :],
                                       start=(k == 0), stop=(k == KC - 1))
                    mm.then_inc(proj_mm, 1)

            skewed(pe, NTILE, 2, OB, step)

        @block.scalar
        def _(act):
            act.sem_inc(attn_t_ready, ATT_0)
            with act.Fori(0, NTILE // 2) as i:
                for p in range(2):
                    n = i * 2 + p
                    act.wait_ge(a_tr_mm, n + (ATR_0 + 1))
                    act.wait_ge(proj_mm, n + (PROJ_0 - 1))
                    act.activation(attn_t[:, p, :], a_tr_ps[:, p, 0:D], ACT.Copy).then_inc(attn_t_ready, 1)
            act.wait_ge(var_ready, 1)
            act.activation(rstd2[:, :], rstd2[:, :], ACT.Sqrt).then_inc(std_ready, 1)

        @block.gpsimd
        def _(pool):
            pool.sem_inc(x1_ready, X1_0)
            pool.wait_ge(x_in, 16)
            with pool.Fori(0, NTILE) as n:
                pool.wait_ge(gated_ready, n + (GATED_0 + 1))
                x1 = x1_sb[:, ds(n * D, D)]
                pool.tensor_tensor(x1, x1, gated[:, :], ALU.add).then_inc(x1_ready, 1)

        @block.vector
        def _(dve):
            dve.sem_inc(attn_ready, ATTN_0)
            dve.sem_inc(gated_ready, GATED_0)
            dve.memset(zeros[:, :], 0.0).then_inc(zero_ready, 1)
            dve.wait_ge(x_in, 16)

            def step(m, u, active):
                if active(0):
                    heads = o_tr_ps[:, u % 2, :].rearrange("p (h v) -> p h v", v=VW)
                    dve.wait_ge(o_tr_mm, m + (OTR_0 + 1))
                    dve.wait_ge(a_tr_mm, m + (ATR_0 - 1))
                    dve.wait_ge(attn_ready, m + ATTN_0)
                    dve.reciprocal(rden[:, :], heads[:, :, HD]).then_inc(rden_ready, 1)
                    dve.wait_ge(rden_ready, m + 1)
                    dve.tensor_tensor(attn[:, u % 2, :].rearrange("p (h d) -> p h d", d=HD), heads[:, :, 0:HD],
                                      rden[:, :].rearrange("p (h o) -> p h o", o=1).broadcast_to([P, H, HD]),
                                      ALU.mult).then_inc(attn_ready, 1)
                if active(2):
                    n = m - 2
                    dve.wait_ge(proj_mm, n + (PROJ_0 + 1))
                    dve.wait_ge(x1_ready, n + X1_0)
                    gate = modrow[:, ds(n // (NBLK * TPB) * (6 * D) + 2 * D, D)]
                    dve.tensor_tensor(gated[:, :], proj_ps[:, u % 2, 0:D], gate, ALU.mult).then_inc(gated_ready, 1)
                if active(3):
                    n = m - 3
                    dve.wait_ge(x1_ready, n + (X1_0 + 1))
                    dve.bn_stats(bn[:, ds(n * 6, 6)], x1_sb[:, ds(n * D, D)]).then_inc(stats_ready, 1)

            skewed(dve, NTILE, 3, 2, step)
            dve.wait_ge(stats_ready, NTILE)
            for n in range(NTILE):
                last = dve.bn_aggr(stats2[:, 2 * n:2 * n + 2], bn[:, 6 * n:6 * n + 6])
            last.then_inc(stats_ready, 1)
            dve.wait_ge(stats_ready, NTILE + 1)
            pairs = stats2[:, :].rearrange("p (n s) -> p n s", s=2)
            dve.tensor_scalar(rstd2[:, :], pairs[:, :, 1], EPS, None, ALU.add).then_inc(var_ready, 1)
            dve.wait_ge(std_ready, 1)
            dve.reciprocal(rstd2[:, :], rstd2[:, :]).then_inc(var_ready, 1)
            dve.wait_ge(var_ready, 2)
            dve.scalar_tensor_tensor(pairs[:, :, 0], pairs[:, :, 0], -1.0, rstd2[:, :], ALU.mult, ALU.mult)


def stage_router(nc, a, dram, modrow, ident, x1_sb, h2_sb, stats2, rstd2, top_logit, top_index, scattered):
    with ExitStack() as ctx:
        sb = lambda n, s, dt=F32: ctx.enter_context(nc.sbuf_tensor(n, s, dt))
        ps = lambda n, s: ctx.enter_context(nc.psum_tensor(n, s, F32))
        sem = lambda n: ctx.enter_context(nc.semaphore(n))
        HC = HID // P
        SLOTS = TPB * TOPK
        rw1 = sb("rw1", [P, KC * HID])
        rw1_hi = sb("rw1_hi", [P, KC * HID], F32R)
        rw1_lo = sb("rw1_lo", [P, KC * HID], F32R)
        rw2 = sb("rw2", [P, HC, LW])
        rb1 = sb("rb1", [P, HC])
        rb2 = sb("rb2", [P, E])
        before = sb("r_before", [P, P])
        all_ones = sb("r_ones", [P, P])
        expert_iota = sb("r_iota", [P, E])
        region_base = sb("region_base", [P, E])
        xn = sb("xn2", [P, 2, D])
        h2_blk = sb("h2_blk", [P, 2, TPB, D])
        h2_hi = sb("h2_hi", [P, 2, KC, BLK], F32R)
        h2_lo = sb("h2_lo", [P, 2, KC, BLK], F32R)
        act_t = sb("act_t", [P, 2, HC, BLK])
        log_sb = sb("log_sb", [P, P])
        logits = sb("logits", [P, TPB, E])
        top8 = sb("top8", [P, TPB, E])
        index8 = sb("index8", [P, TPB, E], U32)
        index_f = sb("index_f", [P, TPB, TOPK])
        hot = sb("r_hot", [P, TPB, TOPK, E])
        both = sb("r_both", [P, TPB, E])
        seen = sb("seen", [P, TPB + 1, E])
        row = sb("r_row", [P, TPB, E])
        picked = sb("r_picked", [P, TPB, TOPK, E])
        place_f = sb("place_f", [P, SLOTS])
        place = sb("place", [P, NTILE * TOPK], U32)
        HB = 3
        tr_ps = ps("tr_ps", [P, KC, BLK])
        hid_ps = ps("hid_ps", [P, HB, BLK])
        log_ps = ps("log_ps", [P, BLK])
        lgt_ps = ps("lgt_ps", [P, BLK])
        rank_ps = ps("rank_ps", [P, BLK])
        waited = sem("r_waited")
        w_in, x1_stored, h2_kept = sem("rw_in"), sem("x1_stored"), sem("h2_kept")
        rw2_ready, rw1_split = sem("rw2_ready"), sem("rw1_split")
        ln_step, h2_ready, tr_mm, h2_t_step, hid_mm, act_ready, log_mm, log_ready, lgt_mm = (
            sem("ln_step"), sem("h2_ready"), sem("tr_mm"), sem("h2_t_step"), sem("hid_mm"), sem("act_ready"),
            sem("log_mm"), sem("log_ready"), sem("lgt_mm"))
        logit_ready, top_ready, index_ready, kept, rank_step, rank_mm, row_step, place_ready = (
            sem("logit_ready"), sem("top_ready"), sem("index_ready"), sem("kept"), sem("rank_step"),
            sem("rank_mm"), sem("row_step"), sem("place_ready"))
        block = ctx.enter_context(nc.Block())
        H2T_0, ACT_0, LOG_0, HIDM_0, LOGM_0, TR_0, H2K_0, H2_0, PL_0 = 2, HC, 1, 2 * HC, 2, 2, 2, 1, 1
        N_RANK = TPB + 4
        N_ROW = 4
        bank_before = lambda hc: hc - HB if hc >= HB else max(
            h for h in range(HC) if h % HB == hc % HB) - HC

        @block.sync
        def _(sp):
            sp.dma_start(rw1[:, :].rearrange("p (k n) -> p k n", k=KC),
                         a["rw1"].rearrange("(k p) n -> p k n", p=P)).then_inc(w_in, 16)
            sp.dma_start(rb1[:, :], a["rb1_cols"]).then_inc(w_in, 16)
            sp.dma_start(rb2[:, :], a["rb2"].partition_broadcast(P)).then_inc(w_in, 16)
            sp.dma_start(before[:, :], a["before"]).then_inc(w_in, 16)
            sp.dma_start(all_ones[:, :], a["ones"]).then_inc(w_in, 16)
            sp.dma_start(expert_iota[:, :], a["iota"][0:E].partition_broadcast(P)).then_inc(w_in, 16)
            sp.dma_start(region_base[:, :], a["region_base"].partition_broadcast(P)).then_inc(w_in, 16)
            sp.wait_ge(rw2_ready, 1)
            sp.dma_start(rw2[:, :, 0:E], a["rw2"].rearrange("(c p) e -> p c e", p=P)).then_inc(w_in, 16)
            sp.dma_start(dram["x1"].rearrange("(n p) d -> p n d", p=P),
                         x1_sb[:, :].rearrange("p (n d) -> p n d", d=D)).then_inc(x1_stored, 16)
            sp.wait_ge(x1_stored, 16)

        @block.tensor
        def _(pe):
            def step(m, u, active):
                if active(4):
                    pe.wait_ge(log_ready, m - 4 + (LOG_0 + 1))
                    pe.transpose(lgt_ps[:, 0:P], log_sb[:, :], ident[:, :]).then_inc(lgt_mm, 1)
                if active(5):
                    n = m - 5
                    pe.wait_ge(rank_step, n * N_RANK + N_RANK)
                    flat = lambda t: t.rearrange("p t e -> p (t e)")
                    pe.matmul(rank_ps[:, 0:TPB * E], before[:, :], flat(both[:, :, :]), start=True, stop=False)
                    pe.matmul(rank_ps[:, 0:TPB * E], all_ones[:, :], flat(seen[:, 0:TPB, :]),
                              start=False, stop=True).then_inc(rank_mm, 1)
                if active(3):
                    n, p = m - 3, (u - 3) % 2
                    pe.wait_ge(act_ready, n * HC + (HC + ACT_0))
                    pe.wait_ge(log_ready, n + LOG_0)
                    for hc in range(HC):
                        for t in range(TPB):
                            mm = pe.matmul(log_ps[t * LW:(t + 1) * LW, 0:P], rw2[:, hc, :],
                                           act_t[:, p, hc, t * P:(t + 1) * P],
                                           start=(hc == 0), stop=(hc == HC - 1))
                    mm.then_inc(log_mm, 1)
                if active(1):
                    n, p = m - 1, (u - 1) % 2
                    pe.wait_ge(h2_ready, n * TPB + (TPB + H2_0))
                    pe.wait_ge(h2_t_step, n * 2 + H2T_0)
                    for t in range(TPB):
                        for k in range(KC):
                            tr = pe.transpose(tr_ps[:, k, t * P:(t + 1) * P],
                                              h2_blk[:, p, t, k * P:(k + 1) * P], ident[:, :])
                    tr.then_inc(tr_mm, 1)
                if active(2):
                    n, p = m - 2, u % 2
                    pe.wait_ge(h2_t_step, n * 2 + (H2T_0 + 2))
                    for hc in range(HC):
                        pe.wait_ge(act_ready, n * HC + (bank_before(hc) + 1 + ACT_0))
                        terms = [(w, x, k) for w, x in ((rw1_hi, h2_hi), (rw1_hi, h2_lo), (rw1_lo, h2_hi))
                                 for k in range(KC)]
                        for j, (w, x, k) in enumerate(terms):
                            mm = pe.matmul(hid_ps[:, hc % HB, :], w[:, k * HID + hc * P:k * HID + (hc + 1) * P],
                                           x[:, p, k, :], start=(j == 0), stop=(j == len(terms) - 1))
                        mm.then_inc(hid_mm, 1)

            pe.sem_inc(log_mm, LOGM_0)
            pe.sem_inc(tr_mm, TR_0)
            pe.sem_inc(hid_mm, HIDM_0)
            pe.wait_ge(w_in, 128)
            pe.wait_ge(rw1_split, 2)
            skewed(pe, N_RBLK, 5, 2, step)

        @block.scalar
        def _(act):
            act.sem_inc(act_ready, ACT_0)
            act.sem_inc(h2_kept, H2K_0)
            act.wait_ge(w_in, 128)

            def step(m, u, active):
                if active(2):
                    n, p = m - 2, u % 2
                    act.wait_ge(log_mm, n + (LOGM_0 - 1))
                    for hc in range(HC):
                        act.wait_ge(hid_mm, n * HC + (hc + 1 + HIDM_0))
                        act.activation(act_t[:, p, hc, :], hid_ps[:, hc % HB, :], ACT.Silu,
                                       bias=rb1[:, hc:hc + 1]).then_inc(act_ready, 1)
                if active(0):
                    act.wait_ge(h2_ready, m * TPB + (TPB + H2_0))
                    act.activation(h2_sb[:, ds(m * (TPB * D), TPB * D)],
                                   h2_blk[:, u % 2, :, :].rearrange("p t d -> p (t d)"), ACT.Copy
                                   ).then_inc(h2_kept, 1)

            skewed(act, N_RBLK, 2, 2, step)

        @block.gpsimd
        def _(pool):
            for n in range(N_RBLK):
                pool.wait_ge(h2_kept, n + 1 + H2K_0)
                pool.wait_ge(place_ready, n + 1 + PL_0)
                for t in range(TPB):
                    for s in range(TOPK):
                        tile = n * TPB + t
                        j = tile * TOPK + s
                        pool.indirect_dma_start(dram["x_rows"],
                                                bass.IndirectOffsetOnAxis(ap=place[:, j:j + 1], axis=0),
                                                h2_sb[:, tile * D:(tile + 1) * D], None).then_inc(scattered, 16)

        @block.vector
        def _(dve):
            def place_rows(n):
                dve.wait_ge(rank_mm, n + 1)
                dve.tensor_tensor(row[:, :, :], rank_ps[:, 0:TPB * E].rearrange("p (t e) -> p t e", e=E),
                                  region_base[:, :].rearrange("p (o e) -> p o e", o=1).broadcast_to([P, TPB, E]),
                                  ALU.add).then_inc(row_step, 1)
                dve.wait_ge(row_step, n * N_ROW + 1)
                for s in range(TOPK):
                    dve.tensor_tensor(picked[:, :, s, :], hot[:, :, s, :], row[:, :, :], ALU.mult
                                      ).then_inc(row_step, 1)
                dve.wait_ge(row_step, n * N_ROW + 3)
                dve.wait_ge(place_ready, n + PL_0)
                dve.sem_inc(waited, 1)
                dve.tensor_reduce(place_f[:, :], picked[:, :, :, :].rearrange("p t s e -> p (t s) e"), AX_X,
                                  ALU.add).then_inc(row_step, 1)
                dve.wait_ge(row_step, n * N_ROW + 4)
                dve.tensor_copy(place[:, ds(n * SLOTS, SLOTS)], place_f[:, :]).then_inc(place_ready, 1)

            def choose(n):
                dve.wait_ge(lgt_mm, n + 1)
                dve.tensor_tensor(logits[:, :, :], lgt_ps[:, 0:P].rearrange("p (t e) -> p t e", e=LW)[:, :, 0:E],
                                  rb2[:, :].rearrange("p (o e) -> p o e", o=1).broadcast_to([P, TPB, E]),
                                  ALU.add).then_inc(logit_ready, 1)
                dve.wait_ge(logit_ready, n + 1)
                dve.wait_ge(kept, n + 1)
                dve.sem_inc(waited, 1)
                for t in range(TPB):
                    dve.max(top8[:, t, :], logits[:, t, :]).then_inc(top_ready, 1)
                dve.wait_ge(top_ready, n * TPB + TPB)
                dve.sem_inc(waited, 1)
                for t in range(TPB):
                    dve.max_index(index8[:, t, :], top8[:, t, :], logits[:, t, :]).then_inc(index_ready, 1)
                dve.wait_ge(index_ready, n * TPB + TPB)
                dve.tensor_copy(top_logit[:, ds(n * SLOTS, SLOTS)].rearrange("p (t s) -> p t s", s=TOPK),
                                top8[:, :, 0:TOPK]).then_inc(kept, 1)
                dve.tensor_copy(index_f[:, :, :], index8[:, :, 0:TOPK]).then_inc(rank_step, 1)
                dve.wait_ge(rank_step, n * N_RANK + 1)
                dve.tensor_copy(top_index[:, ds(n * SLOTS, SLOTS)],
                                index_f[:, :, :].rearrange("p t s -> p (t s)"))
                dve.tensor_tensor(hot[:, :, :, :].rearrange("p t s e -> p (t s) e"),
                                  index_f[:, :, :].rearrange("p t (s o) -> p (t s) o", o=1
                                                             ).broadcast_to([P, SLOTS, E]),
                                  expert_iota[:, :].rearrange("p (o e) -> p o e", o=1).broadcast_to([P, SLOTS, E]),
                                  ALU.is_equal).then_inc(rank_step, 1)
                dve.tensor_copy(seen[:, 0, :], seen[:, TPB, :]).then_inc(rank_step, 1)
                dve.wait_ge(rank_step, n * N_RANK + 3)
                dve.tensor_tensor(both[:, :, :], hot[:, :, 0, :], hot[:, :, 1, :], ALU.add).then_inc(rank_step, 1)
                for t in range(TPB):
                    dve.wait_ge(rank_step, n * N_RANK + (4 + t))
                    dve.tensor_tensor(seen[:, t + 1, :], seen[:, t, :], both[:, t, :], ALU.add
                                      ).then_inc(rank_step, 1)

            def normalise(m, u):
                dve.wait_ge(tr_mm, m + (TR_0 - 1))
                dve.wait_ge(h2_kept, m + (H2K_0 - 1))
                for t in range(TPB):
                    tile = m * TPB + t
                    mod = m // NBLK * (6 * D)
                    dve.tensor_scalar(xn[:, 0, :], x1_sb[:, ds(tile * D, D)], rstd2[:, ds(tile, 1)],
                                      stats2[:, ds(tile * 2, 1)], ALU.mult, ALU.add).then_inc(ln_step, 1)
                    dve.wait_ge(ln_step, tile * 2 + 1)
                    dve.wait_ge(h2_ready, tile + H2_0)
                    dve.tensor_tensor(xn[:, 1, :], xn[:, 0, :], modrow[:, ds(mod + 4 * D, D)],
                                      ALU.mult).then_inc(ln_step, 1)
                    dve.wait_ge(ln_step, tile * 2 + 2)
                    dve.tensor_tensor(h2_blk[:, u % 2, t, :], xn[:, 1, :], modrow[:, ds(mod + 3 * D, D)],
                                      ALU.add).then_inc(h2_ready, 1)

            def step(m, u, active):
                if active(5):
                    place_rows(m - 5)
                if active(4):
                    choose(m - 4)
                if active(3):
                    n = m - 3
                    dve.wait_ge(log_mm, n + (LOGM_0 + 1))
                    dve.tensor_copy(log_sb[:, :], log_ps[:, 0:P]).then_inc(log_ready, 1)
                if active(1):
                    n, p = m - 1, (u - 1) % 2
                    dve.wait_ge(tr_mm, n + (TR_0 + 1))
                    dve.wait_ge(hid_mm, n * HC + (HIDM_0 - HC))
                    dve.tensor_copy(h2_hi[:, p, :, :], tr_ps[:, :, :]).then_inc(h2_t_step, 1)
                    dve.wait_ge(h2_t_step, n * 2 + (H2T_0 + 1))
                    dve.tensor_tensor(h2_lo[:, p, :, :], tr_ps[:, :, :], h2_hi[:, p, :, :].bitcast(F32),
                                      ALU.subtract).then_inc(h2_t_step, 1)
                if active(0):
                    normalise(m, u)

            dve.memset(rw2[:, :, :], 0.0).then_inc(rw2_ready, 1)
            dve.sem_inc(h2_ready, H2_0)
            dve.sem_inc(h2_t_step, H2T_0)
            dve.sem_inc(log_ready, LOG_0)
            dve.sem_inc(place_ready, PL_0)
            dve.memset(seen[:, :, :], 0.0).then_inc(kept, 1)
            dve.wait_ge(w_in, 128)
            dve.tensor_copy(rw1_hi[:, :], rw1[:, :]).then_inc(rw1_split, 1)
            dve.wait_ge(rw1_split, 1)
            dve.tensor_tensor(rw1_lo[:, :], rw1[:, :], rw1_hi[:, :].bitcast(F32), ALU.subtract
                              ).then_inc(rw1_split, 1)
            skewed(dve, N_RBLK, 5, 2, step)


def stage_dispatch(nc, a, dram, top_logit, top_index, prob, slot_row, tile_expert, tile_row, zeros,
                   scattered, w1, w2, b2, weights_in):
    with ExitStack() as ctx:
        sb = lambda n, s, dt=F32: ctx.enter_context(nc.sbuf_tensor(n, s, dt))
        ps = lambda n, s: ctx.enter_context(nc.psum_tensor(n, s, F32))
        sem = lambda n: ctx.enter_context(nc.semaphore(n))
        NS = NTILE * TOPK
        before = sb("before", [P, P])
        all_ones = sb("all_ones", [P, P])
        expert_iota = sb("expert_iota", [P, E])
        tile_iota = sb("tile_iota", [P, NET])
        hot = sb("hot", [P, NS, E])
        both = sb("both", [P, NTILE, E])
        total = sb("total", [P, 2, NTILE, E])
        count = sb("count", [P, E])
        count_i = sb("count_i", [P, E], U32)
        padded = sb("padded", [P, E])
        start = sb("start", [P, 2, E])
        row = sb("row", [P, NTILE, E])
        picked = sb("picked", [P, NS, E])
        slot_f = sb("slot_f", [P, NS])
        passed = sb("passed", [P, NET, E])
        expert_f = sb("expert_f", [P, NET])
        skipped = sb("skipped", [P, E])
        row_f = sb("row_f", [P, NET])
        pad_base = sb("pad_base", [P, E])
        pad_row = sb("pad_row", [P, E], U32)
        diff = sb("diff", [P, NTILE])
        ediff = sb("ediff", [P, NTILE])
        denom = sb("denom", [P, NTILE])
        pre_ps = ps("pre_ps", [P, NTILE * E])
        tot_ps = ps("tot_ps", [P, NTILE * E])
        c_in, both_ready, sums_mm, diff_ready, exp_ready, pads_ready, chain = (
            sem("dc_in"), sem("both_ready"), sem("sums_mm"), sem("diff_ready"), sem("exp_ready3"),
            sem("pads_ready"), sem("dispatch_chain"))
        block = ctx.enter_context(nc.Block())

        @block.sync
        def _(sp):
            sp.dma_start(before[:, :], a["before"]).then_inc(c_in, 16)
            sp.dma_start(all_ones[:, :], a["ones"]).then_inc(c_in, 16)
            sp.dma_start(expert_iota[:, :], a["iota"][0:E].partition_broadcast(P)).then_inc(c_in, 16)
            sp.dma_start(tile_iota[:, :], a["iota"].partition_broadcast(P)).then_inc(c_in, 16)
            sp.dma_start(pad_base[:, :], a["pad_base"]).then_inc(c_in, 16)
            w1v = w1[:, :].rearrange("p (e k n) -> p e k n", e=E, k=KC)
            w2v = w2[:, :].rearrange("p (e c n) -> p e c n", e=E, c=HID // P)
            for e in range(E):
                sp.dma_start(w1v[:, e], a["w1"][e].rearrange("(k p) n -> p k n", p=P)).then_inc(weights_in, 16)
                sp.dma_start(w2v[:, e], a["w2"][e].rearrange("(c p) n -> p c n", p=P)).then_inc(weights_in, 16)
            sp.dma_start(b2[:, :], a["b2"].partition_broadcast(P)).then_inc(weights_in, 16)

        @block.tensor
        def _(pe):
            pe.wait_ge(both_ready, 1)
            flat = both[:, :, :].rearrange("p n e -> p (n e)")
            pe.matmul(pre_ps[:, :], before[:, :], flat, start=True, stop=True)
            pe.matmul(tot_ps[:, :], all_ones[:, :], flat, start=True, stop=True).then_inc(sums_mm, 1)

        @block.scalar
        def _(act):
            act.wait_ge(diff_ready, 1)
            act.activation(ediff[:, :], diff[:, :], ACT.Exp).then_inc(exp_ready, 1)

        @block.vector
        def _(dve):
            done = [0]

            def then_wait(ins):
                done[0] += 1
                ins.then_inc(chain, 1)
                dve.wait_ge(chain, done[0])

            wide = lambda ap, shape: ap.broadcast_to(shape)
            dve.wait_ge(c_in, 80)
            pairs = top_logit[:, :].rearrange("p (n s) -> p n s", s=TOPK)
            dve.tensor_tensor(diff[:, :], pairs[:, :, 1], pairs[:, :, 0], ALU.subtract).then_inc(diff_ready, 1)
            then_wait(dve.tensor_tensor(hot[:, :, :],
                                        wide(top_index[:, :].rearrange("p (n o) -> p n o", o=1), [P, NS, E]),
                                        wide(expert_iota[:, :].rearrange("p (o e) -> p o e", o=1), [P, NS, E]),
                                        ALU.is_equal))
            slots = hot[:, :, :].rearrange("p (n s) e -> p n s e", s=TOPK)
            dve.tensor_tensor(both[:, :, :], slots[:, :, 0, :], slots[:, :, 1, :], ALU.add).then_inc(both_ready, 1)
            dve.wait_ge(sums_mm, 1)
            then_wait(dve.tensor_copy(total[:, 0, :, :], tot_ps[:, :].rearrange("p (n e) -> p n e", e=E)))
            cur = 0
            for d in (1, 2, 4, 8, 16):
                dve.tensor_copy(total[:, 1 - cur, 0:d, :], total[:, cur, 0:d, :])
                then_wait(dve.tensor_tensor(total[:, 1 - cur, d:, :], total[:, cur, d:, :],
                                            total[:, cur, 0:NTILE - d, :], ALU.add))
                cur = 1 - cur
            dve.tensor_tensor(pad_row[:, :], total[:, cur, NTILE - 1, :], pad_base[:, :], ALU.add
                              ).then_inc(pads_ready, 1)
            then_wait(dve.tensor_scalar(count[:, :], total[:, cur, NTILE - 1, :], float(P - 1), None, ALU.add))
            then_wait(dve.tensor_copy(count_i[:, :], count[:, :]))
            then_wait(dve.tensor_scalar(count_i[:, :], count_i[:, :], 7, 7, ALU.logical_shift_right,
                                        ALU.logical_shift_left))
            then_wait(dve.tensor_copy(padded[:, :], count_i[:, :]))
            then_wait(dve.tensor_copy(start[:, 0, :], padded[:, :]))
            side = 0
            for d in (1, 2, 4):
                dve.tensor_copy(start[:, 1 - side, 0:d], start[:, side, 0:d])
                then_wait(dve.tensor_tensor(start[:, 1 - side, d:], start[:, side, d:],
                                            start[:, side, 0:E - d], ALU.add))
                side = 1 - side
            ends = start[:, side, :]
            then_wait(dve.tensor_scalar(tile_iota[:, :], tile_iota[:, :], float(P), None, ALU.mult))
            then_wait(dve.tensor_tensor(passed[:, :, :],
                                        wide(tile_iota[:, :].rearrange("p (n o) -> p n o", o=1), [P, NET, E]),
                                        wide(ends.rearrange("p (o e) -> p o e", o=1), [P, NET, E]), ALU.is_ge))
            then_wait(dve.tensor_reduce(expert_f[:, :], passed[:, :, :], AX_X, ALU.add))
            dve.tensor_scalar(tile_expert[:, :], expert_f[:, :], float(E - 1), None, ALU.min)
            then_wait(dve.tensor_scalar(skipped[:, :], padded[:, :], -1.0, float(REGION), ALU.mult, ALU.add))
            then_wait(dve.tensor_tensor(passed[:, :, :], passed[:, :, :],
                                        wide(skipped[:, :].rearrange("p (o e) -> p o e", o=1), [P, NET, E]),
                                        ALU.mult))
            then_wait(dve.tensor_reduce(row_f[:, :], passed[:, :, :], AX_X, ALU.add))
            then_wait(dve.tensor_tensor(row_f[:, :], row_f[:, :], tile_iota[:, :], ALU.add))
            dve.tensor_scalar(tile_row[:, :], row_f[:, :], float(VOID), None, ALU.min)
            then_wait(dve.tensor_tensor(start[:, 1 - side, :], ends, padded[:, :], ALU.subtract))
            then_wait(dve.tensor_tensor(row[:, :, :], pre_ps[:, :].rearrange("p (n e) -> p n e", e=E),
                                        wide(start[:, 1 - side, :].rearrange("p (o e) -> p o e", o=1),
                                             [P, NTILE, E]), ALU.add))
            then_wait(dve.tensor_tensor(row[:, 1:, :], row[:, 1:, :], total[:, cur, 0:NTILE - 1, :], ALU.add))
            for s in range(TOPK):
                dst = picked[:, :, :].rearrange("p (n s) e -> p n s e", s=TOPK)[:, :, s, :]
                then_wait(dve.tensor_tensor(dst, slots[:, :, s, :], row[:, :, :], ALU.mult))
            then_wait(dve.tensor_reduce(slot_f[:, :], picked[:, :, :], AX_X, ALU.add))
            dve.tensor_copy(slot_row[:, :], slot_f[:, :])
            dve.wait_ge(exp_ready, 1)
            then_wait(dve.tensor_scalar(denom[:, :], ediff[:, :], 1.0, None, ALU.add))
            then_wait(dve.reciprocal(denom[:, :], denom[:, :]))
            probs = prob[:, :].rearrange("p (n s) -> p n s", s=TOPK)
            dve.tensor_copy(probs[:, :, 0], denom[:, :])
            then_wait(dve.tensor_tensor(probs[:, :, 1], denom[:, :], ediff[:, :], ALU.mult))

        @block.gpsimd
        def _(pool):
            pool.wait_ge(pads_ready, 1)
            for e in range(E):
                pool.indirect_dma_start(dram["x_rows"], bass.IndirectOffsetOnAxis(ap=pad_row[:, e:e + 1], axis=0),
                                        zeros[:, :], None).then_inc(scattered, 16)
            pool.wait_ge(scattered, 16 * (NS + E))


def stage_experts(nc, a, dram, ident, tile_expert, tile_row, w1, w2, b1, b2, weights_in):
    with ExitStack() as ctx:
        sb = lambda n, s, dt=F32: ctx.enter_context(nc.sbuf_tensor(n, s, dt))
        ps = lambda n, s: ctx.enter_context(nc.psum_tensor(n, s, F32))
        sem = lambda n: ctx.enter_context(nc.semaphore(n))
        HC = HID // P
        rows = sb("rows", [P, 2, D])
        rows_t = sb("rows_t", [P, 2, D])
        hid = sb("hid", [P, 2, HID])
        hid_t = sb("hid_t", [P, 2, HID])
        y = sb("y", [P, 2, D])
        x_tr_ps = ps("x_tr_ps", [P, BLK])
        fc1_ps = ps("fc1_ps", [P, HID])
        h_tr_ps = ps("h_tr_ps", [P, HID])
        fc2_ps = ps("fc2_ps", [P, BLK])
        b1_in = sem("b1_in")
        rows_in = [sem(f"rows_in{p}") for p in range(2)]
        y_stored = [sem(f"y_stored{p}") for p in range(2)]
        x_tr_mm, rows_t_ready, fc1_mm, hid_ready, h_tr_mm, hid_t_ready, fc2_mm, y_ready = (
            sem("x_tr_mm"), sem("rows_t_ready"), sem("fc1_mm"), sem("hid_ready"), sem("h_tr_mm"),
            sem("hid_t_ready"), sem("fc2_mm"), sem("y_ready"))
        block = ctx.enter_context(nc.Block())
        XTR_0, RT_0, FC1_0, HID_0, HTR_0, HT_0, FC2_0, Y_0, ST_0 = 2, 1, 2, 1, 2, 1, 2, 1, 16

        @block.sync
        def _(sp):
            for s in y_stored:
                sp.sem_inc(s, ST_0)
            sp.dma_start(b1[:, :], a["b1"].partition_broadcast(P)).then_inc(b1_in, 16)

            def step(m, u, active):
                if active(0):
                    sp.wait_ge(x_tr_mm, m + (XTR_0 - 1))
                    row = sp.value_load(tile_row[0:1, ds(m, 1)], min_val=0, max_val=VOID)
                    sp.dma_start(rows[:, u % 2, :], dram["x_rows"][ds(row, P), :]).then_inc(rows_in[u % 2], 16)
                if active(4):
                    n = m - 4
                    sp.wait_ge(y_ready, n + (Y_0 + 1))
                    sp.dma_start(dram["y_rows"][ds(n * P, P), :], y[:, u % 2, :]).then_inc(y_stored[u % 2], 16)

            skewed(sp, NET, 4, 2, step)
            for s in y_stored:
                sp.wait_ge(s, ST_0 + 16 * (NET // 2))

        @block.tensor
        def _(pe):
            pe.sem_inc(x_tr_mm, XTR_0)
            pe.sem_inc(fc1_mm, FC1_0)
            pe.sem_inc(h_tr_mm, HTR_0)
            pe.sem_inc(fc2_mm, FC2_0)
            pe.wait_ge(weights_in, 16 * (2 * E + 1))

            def expert_of(n):
                return pe.value_load(tile_expert[0:1, ds(n, 1)], min_val=0, max_val=E - 1)

            def step(m, u, active):
                if active(0):
                    pe.wait_ge(rows_in[u % 2], (m // 2) * 16 + 16)
                    pe.wait_ge(rows_t_ready, m + RT_0)
                    for k in range(KC):
                        tr = pe.transpose(x_tr_ps[:, k * P:(k + 1) * P], rows[:, u % 2, k * P:(k + 1) * P],
                                          ident[:, :])
                    tr.then_inc(x_tr_mm, 1)
                if active(1):
                    n, p = m - 1, (u - 1) % 2
                    e = expert_of(n)
                    pe.wait_ge(rows_t_ready, n + (RT_0 + 1))
                    pe.wait_ge(hid_ready, n + HID_0)
                    for half in range(HID // BLK):
                        for k in range(KC):
                            mm = pe.matmul(fc1_ps[:, half * BLK:(half + 1) * BLK], rows_t[:, p, k * P:(k + 1) * P],
                                           w1[:, ds(e * (KC * HID) + (k * HID + half * BLK), BLK)],
                                           start=(k == 0), stop=(k == KC - 1))
                    mm.then_inc(fc1_mm, 1)
                if active(2):
                    n, p = m - 2, u % 2
                    pe.wait_ge(hid_ready, n + (HID_0 + 1))
                    pe.wait_ge(hid_t_ready, n + HT_0)
                    for hc in range(HC):
                        tr = pe.transpose(h_tr_ps[:, hc * P:(hc + 1) * P], hid[:, p, hc * P:(hc + 1) * P],
                                          ident[:, :])
                    tr.then_inc(h_tr_mm, 1)
                if active(3):
                    n, p = m - 3, (u - 3) % 2
                    e = expert_of(n)
                    pe.wait_ge(hid_t_ready, n + (HT_0 + 1))
                    pe.wait_ge(y_ready, n + Y_0)
                    for hc in range(HC):
                        mm = pe.matmul(fc2_ps[:, 0:D], hid_t[:, p, hc * P:(hc + 1) * P],
                                       w2[:, ds(e * (HC * D) + hc * D, D)], start=(hc == 0), stop=(hc == HC - 1))
                    mm.then_inc(fc2_mm, 1)

            skewed(pe, NET, 3, 2, step)

        @block.scalar
        def _(act):
            act.sem_inc(hid_t_ready, HT_0)

            def step(m, u, active):
                if active(2):
                    n, p = m - 2, u % 2
                    act.wait_ge(h_tr_mm, n + (HTR_0 + 1))
                    act.wait_ge(fc2_mm, n + (FC2_0 - 1))
                    act.activation(hid_t[:, p, :], h_tr_ps[:, :], ACT.Silu).then_inc(hid_t_ready, 1)

            skewed(act, NET, 2, 2, step)

        @block.vector
        def _(dve):
            dve.sem_inc(rows_t_ready, RT_0)
            dve.sem_inc(hid_ready, HID_0)
            dve.sem_inc(y_ready, Y_0)
            dve.wait_ge(weights_in, 16 * (2 * E + 1))
            dve.wait_ge(b1_in, 16)

            def expert_of(n):
                return dve.value_load(tile_expert[0:1, ds(n, 1)], min_val=0, max_val=E - 1)

            def step(m, u, active):
                if active(0):
                    dve.wait_ge(x_tr_mm, m + (XTR_0 + 1))
                    dve.wait_ge(fc1_mm, m + (FC1_0 - 1))
                    dve.tensor_copy(rows_t[:, u % 2, :], x_tr_ps[:, 0:D]).then_inc(rows_t_ready, 1)
                if active(1):
                    n, p = m - 1, (u - 1) % 2
                    e = expert_of(n)
                    dve.wait_ge(fc1_mm, n + (FC1_0 + 1))
                    dve.wait_ge(h_tr_mm, n + (HTR_0 - 1))
                    dve.tensor_tensor(hid[:, p, :], fc1_ps[:, :], b1[:, ds(e * HID, HID)], ALU.add
                                      ).then_inc(hid_ready, 1)
                if active(3):
                    n, p = m - 3, (u - 3) % 2
                    e = expert_of(n)
                    dve.wait_ge(fc2_mm, n + (FC2_0 + 1))
                    dve.wait_ge(y_stored[p], (n // 2) * 16 + ST_0)
                    dve.tensor_tensor(y[:, p, :], fc2_ps[:, 0:D], b2[:, ds(e * D, D)], ALU.add
                                      ).then_inc(y_ready, 1)

            skewed(dve, NET, 3, 2, step)


def stage_combine(nc, a, dram, modrow, prob, slot_row, out):
    with ExitStack() as ctx:
        sb = lambda n, s, dt=F32: ctx.enter_context(nc.sbuf_tensor(n, s, dt))
        sem = lambda n: ctx.enter_context(nc.semaphore(n))
        y_got = sb("y_got", [P, NTILE * TOPK, D])
        x1 = sb("x1_in", [P, NTILE, D])
        mixed = sb("mixed", [P, 2, D])
        gated = sb("gated2", [P, 2, D])
        result = sb("result", [P, NTILE, D])
        x_in = sem("x1_back")
        GT = 4
        gathered = [sem(f"gathered{g}") for g in range(NTILE // GT)]
        step, gated_ready, result_ready, stored = sem("mix_step"), sem("gated_ready2"), sem("result_ready"), sem("stored")
        block = ctx.enter_context(nc.Block())

        @block.gpsimd
        def _(pool):
            for n in range(NTILE):
                for s in range(TOPK):
                    j = n * TOPK + s
                    pool.indirect_dma_start(y_got[:, j, :], None, dram["y_rows"],
                                            bass.IndirectOffsetOnAxis(ap=slot_row[:, j:j + 1], axis=0)
                                            ).then_inc(gathered[n // GT], 16)

        @block.sync
        def _(sp):
            sp.dma_start(x1[:, :, :], dram["x1"].rearrange("(n p) d -> p n d", p=P)).then_inc(x_in, 16)
            half = NTILE // 4
            for q in range(4):
                sp.wait_ge(result_ready, (q + 1) * half)
                sp.dma_start(out.rearrange("(n p) d -> p n d", p=P)[:, q * half:(q + 1) * half, :],
                             result[:, q * half:(q + 1) * half, :]).then_inc(stored, 16)
            sp.wait_ge(stored, 64)

        @block.vector
        def _(dve):
            dve.wait_ge(x_in, 16)
            for n in range(NTILE):
                gate = modrow[:, (n // (NTILE // B) * 6 + 5) * D:(n // (NTILE // B) * 6 + 6) * D]
                if n % GT == 0:
                    dve.wait_ge(gathered[n // GT], 16 * TOPK * GT)
                dve.tensor_scalar(mixed[:, 0, :], y_got[:, 2 * n, :], prob[:, 2 * n:2 * n + 1], None, ALU.mult
                                  ).then_inc(step, 1)
                dve.wait_ge(step, 3 * n + 1)
                dve.scalar_tensor_tensor(mixed[:, 1, :], y_got[:, 2 * n + 1, :], prob[:, 2 * n + 1:2 * n + 2],
                                         mixed[:, 0, :], ALU.mult, ALU.add).then_inc(step, 1)
                dve.wait_ge(step, 3 * n + 2)
                if n:
                    dve.wait_ge(result_ready, n)
                dve.tensor_tensor(gated[:, 0, :], mixed[:, 1, :], gate, ALU.mult).then_inc(step, 1)
                dve.wait_ge(step, 3 * n + 3)
                dve.tensor_tensor(result[:, n, :], gated[:, 0, :], x1[:, n, :], ALU.add).then_inc(result_ready, 1)


INPUTS = ["x", "c_t", "wmod", "ident", "scalars", "transforms", "transform_weights", "qkv_wt", "code_wt",
          "head_sum", "soft_sum", "out_wt", "rw1", "rw2", "rb1_cols", "rb2", "before", "ones", "iota",
          "region_base", "pad_base",
          "w1", "w2", "b1", "b2"]


def kernel(**inputs):
    import numpy as np
    import concourse.bacc as bacc
    from concourse.bass_utils import run_bass_kernel_spmd

    arr = lambda name: np.asarray(inputs["L0_" + name])
    flat = np.ascontiguousarray
    scalars = [arr("attn_hamming_lambda_logit"), arr("attn_scale_logit"), arr("attn_sips_alpha"),
               arr("attn_sips_beta")]
    given = {
        "x": flat(arr("attn_x").reshape(NTOK, D)),
        "c_t": flat(arr("c").T),
        "wmod": flat(arr("wmod")),
        "scalars": np.concatenate([s.reshape(1) for s in scalars]),
        "transforms": flat(arr("attn_transforms").transpose(1, 0, 2)),
        "transform_weights": flat(arr("attn_transform_weights").reshape(H * NT)),
        "qkv_wt": flat(arr("attn_qkv_w").T),
        "code_wt": flat(np.concatenate([arr("attn_q6_w"), arr("attn_hex_w")]).T),
        "out_wt": flat(arr("attn_out_w").T),
        "rw1": flat(arr("ffn_rw1")),
        "rw2": flat(arr("ffn_rw2")),
        "rb1_cols": flat(arr("ffn_rb1").reshape(HID // P, P).T),
        "rb2": flat(arr("ffn_rb2")),
        "w1": flat(arr("ffn_w1")),
        "w2": flat(arr("ffn_w2")),
        "b1": flat(arr("ffn_b1").reshape(E * HID)),
        "b2": flat(arr("ffn_b2").reshape(E * D)),
        "ident": np.eye(P, dtype=np.float32),
        "head_sum": np.repeat(np.eye(H, dtype=np.float32), HEX, axis=0),
        "soft_sum": np.repeat(np.array([[0.0], [1.0]], np.float32), HEX, axis=0).repeat(H, axis=1),
        "before": np.triu(np.ones((P, P), np.float32), 1),
        "ones": np.ones((P, P), np.float32),
        "iota": np.arange(NET, dtype=np.float32),
        "region_base": np.arange(E, dtype=np.float32) * REGION,
        "pad_base": (np.arange(P)[:, None] + np.arange(E)[None, :] * REGION).astype(np.float32),
    }
    nc = bacc.Bacc("TRN2", target_bir_lowering=False, num_devices=1)
    arrays = {f"in_{name}": given[name] for name in INPUTS}
    a = {name: nc.dram_tensor(f"in_{name}", given[name].shape, F32, kind="ExternalInput").ap() for name in INPUTS}
    out = nc.dram_tensor("out", (NTOK, D), F32, kind="ExternalOutput").ap()
    build(nc, a, out)
    r = run_bass_kernel_spmd(nc, [arrays], core_ids=[0])
    return r.results[0]["out"].reshape(B, T, D)
```

```python
from contextlib import ExitStack

import concourse.bass as bass
from concourse import mybir

ACT = mybir.ActivationFunctionType
ALU = mybir.AluOpType
F32 = mybir.dt.float32
F32R = mybir.dt.float32r
U32 = mybir.dt.uint32
AX_X = mybir.AxisListType.X
ds = bass.ds

P = 128
B, T, D, H, HD, NT, HEX = 2, 2048, 256, 16, 16, 7, 6
NTOK = B * T
HID, E, TOPK = 1024, 8, 2
KC = D // P
BLK = 512
TPB = BLK // P
NBLK = T // BLK
NTILE = NTOK // P
HG = 4
NG = H // HG
NIT = B * NG
ROWS = 64
HROWS = 2 * HEX
BIAS_ROWS = 4 * HROWS + 2
VW = 32
SAFE = 60.0
EPS = 1e-5
TR = 4
NET = -(-(NTOK * TOPK // P + E) // TR) * TR
REGION = NTOK + P
VOID = E * REGION
PAY = D + 4
DIFF_PROB, SECOND_PROB, FIRST_EXPERT, TOKEN = range(D, PAY)
LW = 32
N_RBLK = B * NBLK

def diagonal_steps(qb):
    k = TPB * qb
    late = lambda j, column: (k + j, column, j * P, BLK - j * P)
    return [(qb, [late(0, 0)]), (qb, [late(3, 0), late(1, P)]), (qb, [late(2, 2 * P)])]


assert TPB == 4
STEPS = [step for qb in range(NBLK) for step in
         [(qb, [(kt, 0, 0, BLK)]) for kt in range(TPB * qb)] + diagonal_steps(qb)]
NSTEP = len(STEPS)
LAST_OF = {qb: max(s for s, (q, _) in enumerate(STEPS) if q == qb) for qb in range(NBLK)}
FIRST_OF = {qb: min(s for s, (q, _) in enumerate(STEPS) if q == qb) for qb in range(NBLK)}
LAST_USE = {c: max(s for s, (_, pieces) in enumerate(STEPS) if any(piece[0] // TPB == c for piece in pieces))
            for c in range(NBLK)}
DIAG = [s for s, (qb, pieces) in enumerate(STEPS) if pieces[0][0] >= TPB * qb]
PE_LEAD = 3
DVE_LEAD = 2
NBUF = 4
assert NSTEP % NBUF == 0


def first_column(step):
    return min(column for _, column, _, _ in STEPS[step][1])


def build(nc, a, out):
    dram = {}

    def scratch(name, shape, dt=F32):
        dram[name] = nc.dram_tensor(name, shape, dt, kind="Internal").ap()

    scratch("q_split", (B * H * 2 * HD, T))
    scratch("k_split", (B * H * 2 * HD, T))
    scratch("lat_split", (B * H * 4 * HEX, T))
    scratch("soft_split", (B * 4 * HEX, T))
    scratch("code_split", (B * 2 * 4 * HEX, T))
    scratch("guard_split", (B * H * 2, T))
    scratch("v_rows", (B * T, H * VW))
    scratch("o_t", (NIT * P, T))
    scratch("x_rows", (VOID + P, PAY))

    with ExitStack() as ctx:
        modrow = ctx.enter_context(nc.sbuf_tensor("modrow", [P, B * 6 * D], F32))
        ident = ctx.enter_context(nc.sbuf_tensor("ident", [P, P], F32))
        scal = ctx.enter_context(nc.sbuf_tensor("scal", [P, 16], F32))
        with ExitStack() as c2:
            x_sb = c2.enter_context(nc.sbuf_tensor("x_sb", [P, NTILE * D], F32))
            stats = c2.enter_context(nc.sbuf_tensor("stats", [P, NTILE * 2], F32))
            rstd = c2.enter_context(nc.sbuf_tensor("rstd", [P, NTILE], F32))
            lattice = c2.enter_context(nc.sbuf_tensor("lattice", [HEX, H * HEX], F32))
            stage_modulation(nc, a, modrow, ident, scal, x_sb, stats, rstd, lattice)
            stage_projection(nc, a, dram, modrow, ident, scal, x_sb, lattice)
        rows_sb = ctx.enter_context(nc.sbuf_tensor("rows_sb", [P, NTILE * PAY], F32))
        x_back = ctx.enter_context(nc.semaphore("x_back"))
        stage_attention(nc, a, dram, scal, rows_sb, x_back)
        sb = lambda scope, n, shape, dt=F32: scope.enter_context(nc.sbuf_tensor(n, shape, dt))
        tile_expert = sb(ctx, "tile_expert", [P, NET], U32)
        expert_f = sb(ctx, "expert_f", [P, NET])
        tile_row = sb(ctx, "tile_row", [P, NET], U32)
        token_f = sb(ctx, "token_f", [P, NTILE + 1])
        all_ones = sb(ctx, "all_ones", [P, P])
        pad_base = sb(ctx, "pad_base", [P, E])
        tile_first = sb(ctx, "tile_first", [P, NET])
        blank = sb(ctx, "blank", [P, PAY])
        pad_row = sb(ctx, "pad_row", [P, E], U32)
        w1_in = ctx.enter_context(nc.semaphore("w1_in"))
        w1 = sb(ctx, "w1", [P, E * KC * HID])
        with ExitStack() as c2:
            rw1 = sb(c2, "rw1", [P, KC * HID])
            rw1_hi = sb(c2, "rw1_hi", [P, KC * HID], F32R)
            rw1_lo = sb(c2, "rw1_lo", [P, KC * HID], F32R)
            rw2 = sb(c2, "rw2", [P, HID // P, LW])
            rb1 = sb(c2, "rb1", [P, HID // P])
            rb2 = sb(c2, "rb2", [P, E])
            before = sb(c2, "before", [P, P])
            expert_iota = sb(c2, "expert_iota", [P, E])
            region_base = sb(c2, "region_base", [P, E])
            router_weights = (rw1_hi, rw1_lo, rw2, rb1, rb2, before, all_ones, expert_iota, region_base)
            stats2 = sb(c2, "stats2", [P, NTILE * 2])
            rstd2 = sb(c2, "rstd2", [P, NTILE])
            stage_output(nc, a, dram, modrow, ident, rows_sb, stats2, rstd2, token_f, blank, out,
                         rw1, router_weights, pad_base, tile_first, x_back)
            stage_router(nc, a, dram, modrow, ident, rows_sb, stats2, rstd2, token_f, blank, w1, w1_in, out,
                         router_weights, pad_base, tile_first, tile_expert, expert_f, tile_row, pad_row)
        stage_experts(nc, a, dram, modrow, ident, tile_expert, expert_f, tile_row, w1, w1_in, out)


HAM, SCALE, ALPHA, BETA, SIG_HAM, SIG_SCALE, HALF_LAM, LAT_SCALE, INV_BETA, ROOM = range(10)


def stage_modulation(nc, a, modrow, ident, scal, x_sb, stats, rstd, lattice):
    with ExitStack() as ctx:
        sb = lambda n, s, dt=F32: ctx.enter_context(nc.sbuf_tensor(n, s, dt))
        sem = lambda n: ctx.enter_context(nc.semaphore(n))
        wmod = sb("wmod", [P, KC, 6 * D])
        c_t = sb("c_t", [P, KC, B])
        c_silu = sb("c_silu", [P, KC, B])
        c_wide = sb("c_wide", [P, KC, B, P])
        bn = sb("bn", [P, NTILE, 6])
        shift = sb("shift", [P, NTILE])
        gate = sb("gate", [P, D])
        gate_abs = sb("gate_abs", [P, D])
        gate_sign = sb("gate_sign", [P, D])
        trans = sb("trans", [HEX, NT, HEX])
        tw = sb("tw", [HEX, H, NT])
        tw_max = sb("tw_max", [HEX, H])
        tw_sum = sb("tw_sum", [HEX, H])
        lat_term = sb("lat_term", [HEX, H, HEX])
        mod_ps = ctx.enter_context(nc.psum_tensor("mod_ps", [P, B * 6 * D], F32))
        XQ = 4
        c_in, w_in, small_in = sem("c_in"), sem("w_in"), sem("small_in")
        x_in = [sem(f"x_in{q}") for q in range(XQ)]
        shift_ready = sem("shift_ready")
        silu_done, wide_done, mod_done = sem("silu_done"), sem("wide_done"), sem("mod_done")
        var_ready, std_ready, exp_in_ready, exp_ready = (
            sem("var_ready"), sem("std_ready"), sem("exp_in_ready"), sem("exp_ready"))
        chain = sem("mod_chain")
        block = ctx.enter_context(nc.Block())

        def load_x(sp, q):
            n = NTILE // XQ
            sp.dma_start(x_sb[:, q * n * D:(q + 1) * n * D].rearrange("p (n d) -> p n d", d=D),
                         a["x"].rearrange("(n p) d -> p n d", p=P)[:, q * n:(q + 1) * n, :]).then_inc(x_in[q], 16)

        @block.sync
        def _(sp):
            sp.dma_start(c_t[:, :, :], a["c_t"].rearrange("(k p) b -> p k b", p=P)).then_inc(c_in, 16)
            sp.dma_start(ident[:, :], a["ident"]).then_inc(small_in, 16)
            sp.dma_start(scal[:, 0:4], a["scalars"].partition_broadcast(P)).then_inc(small_in, 16)
            sp.dma_start(trans[:, :, :], a["transforms"]).then_inc(small_in, 16)
            sp.dma_start(tw[:, :, :].rearrange("p h t -> p (h t)"),
                         a["transform_weights"].partition_broadcast(HEX)).then_inc(small_in, 16)
            load_x(sp, 0)
            sp.dma_start(wmod[:, :, :], a["wmod"].rearrange("(k p) n -> p k n", p=P)).then_inc(w_in, 16)
            for q in range(1, XQ):
                load_x(sp, q)

        @block.scalar
        def _(act):
            act.wait_ge(c_in, 16)
            act.activation(c_silu[:, :, :], c_t[:, :, :], ACT.Silu).then_inc(silu_done, 1)
            act.wait_ge(small_in, 64)
            act.activation(scal[:, SIG_HAM:SIG_SCALE + 1], scal[:, HAM:SCALE + 1], ACT.Exp,
                           scale=-1.0).then_inc(exp_ready, 1)
            act.wait_ge(exp_in_ready, 1)
            act.activation(tw[:, :, :], tw[:, :, :], ACT.Exp, scale=2.0).then_inc(exp_ready, 1)
            act.wait_ge(var_ready, 1)
            act.activation(rstd[:, :], rstd[:, :], ACT.Sqrt).then_inc(std_ready, 1)
            act.wait_ge(shift_ready, 1)
            for n in range(NTILE):
                tile = x_sb[:, n * D:(n + 1) * D]
                act.activation(tile, tile, ACT.Identity, bias=shift[:, n:n + 1], scale=rstd[:, n:n + 1])

        @block.tensor
        def _(pe):
            pe.wait_ge(w_in, 16)
            pe.wait_ge(wide_done, 1)
            for b in range(B):
                for n in range(3):
                    col = b * 6 * D + n * BLK
                    for k in range(KC):
                        mm = pe.matmul(mod_ps[:, col:col + BLK], c_wide[:, k, b, :],
                                       wmod[:, k, n * BLK:(n + 1) * BLK], start=(k == 0), stop=(k == KC - 1))
            mm.then_inc(mod_done, 1)

        @block.vector
        def _(dve):
            done = [0]

            def then_wait(ins):
                done[0] += 1
                ins.then_inc(chain, 1)
                dve.wait_ge(chain, done[0])

            dve.wait_ge(silu_done, 1)
            dve.tensor_copy(c_wide[:, :, :, :],
                            c_silu[:, :, :].rearrange("p k (b o) -> p k b o", o=1).broadcast_to([P, KC, B, P])
                            ).then_inc(wide_done, 1)
            dve.wait_ge(small_in, 64)
            then_wait(dve.tensor_reduce(tw_max[:, :], tw[:, :, :], AX_X, ALU.max))
            dve.tensor_tensor(tw[:, :, :], tw[:, :, :],
                              tw_max[:, :].rearrange("p (h o) -> p h o", o=1).broadcast_to([HEX, H, NT]),
                              ALU.subtract).then_inc(exp_in_ready, 1)
            dve.wait_ge(exp_ready, 2)
            then_wait(dve.tensor_scalar(scal[:, SIG_HAM:SIG_SCALE + 1], scal[:, SIG_HAM:SIG_SCALE + 1],
                                        1.0, None, ALU.add))
            then_wait(dve.reciprocal(scal[:, SIG_HAM:SIG_SCALE + 1], scal[:, SIG_HAM:SIG_SCALE + 1]))
            dve.tensor_scalar(scal[:, HALF_LAM:HALF_LAM + 1], scal[:, SIG_HAM:SIG_HAM + 1], 0.5, None, ALU.mult)
            dve.tensor_scalar(scal[:, LAT_SCALE:LAT_SCALE + 1], scal[:, SIG_SCALE:SIG_SCALE + 1],
                              2.0 / 6.0, None, ALU.mult)
            dve.reciprocal(scal[:, INV_BETA:INV_BETA + 1], scal[:, BETA:BETA + 1])
            then_wait(dve.scalar_tensor_tensor(scal[:, ROOM:ROOM + 1], scal[:, ALPHA:ALPHA + 1], -1.0,
                                               scal[:, ALPHA:ALPHA + 1], ALU.mult, ALU.min))
            then_wait(dve.tensor_scalar(scal[:, ROOM:ROOM + 1], scal[:, ROOM:ROOM + 1], SAFE, None, ALU.add))
            then_wait(dve.tensor_reduce(tw_sum[:, :], tw[:, :, :], AX_X, ALU.add))
            then_wait(dve.reciprocal(tw_sum[:, :], tw_sum[:, :]))
            then_wait(dve.tensor_scalar(tw_sum[:, :], tw_sum[:, :], scal[0:HEX, LAT_SCALE:LAT_SCALE + 1], None,
                                        ALU.mult))
            then_wait(dve.tensor_tensor(tw[:, :, :], tw[:, :, :],
                                        tw_sum[:, :].rearrange("p (h o) -> p h o", o=1).broadcast_to([HEX, H, NT]),
                                        ALU.mult))
            lat3 = lattice[:, :].rearrange("p (h e) -> p h e", e=HEX)
            for t in range(NT):
                dst = lat3 if t == 0 else lat_term[:, :, :]
                then_wait(dve.tensor_tensor(dst, trans[:, t:t + 1, :].broadcast_to([HEX, H, HEX]),
                                            tw[:, :, t:t + 1].broadcast_to([HEX, H, HEX]), ALU.mult))
                if t:
                    then_wait(dve.tensor_tensor(lat3, lat3, lat_term[:, :, :], ALU.add))
            for n in range(NTILE):
                if n % (NTILE // XQ) == 0:
                    dve.wait_ge(x_in[n // (NTILE // XQ)], 16)
                last = dve.bn_stats(bn[:, n, :], x_sb[:, n * D:(n + 1) * D])
            then_wait(last)
            for n in range(NTILE):
                last = dve.bn_aggr(stats[:, 2 * n:2 * n + 2], bn[:, n, :])
            then_wait(last)
            dve.tensor_scalar(rstd[:, :], stats[:, :].rearrange("p (n s) -> p n s", s=2)[:, :, 1], EPS, None,
                              ALU.add).then_inc(var_ready, 1)
            dve.wait_ge(std_ready, 1)
            then_wait(dve.reciprocal(rstd[:, :], rstd[:, :]))
            dve.scalar_tensor_tensor(shift[:, :], stats[:, :].rearrange("p (n s) -> p n s", s=2)[:, :, 0], -1.0,
                                     rstd[:, :], ALU.mult, ALU.mult).then_inc(shift_ready, 1)
            dve.wait_ge(mod_done, 1)
            for b in range(B):
                for part in range(6):
                    cols = slice((b * 6 + part) * D, (b * 6 + part + 1) * D)
                    if part % 3 == 0:
                        dve.tensor_copy(modrow[:, cols], mod_ps[:, cols])
                    elif part % 3 == 1:
                        dve.tensor_scalar(modrow[:, cols], mod_ps[:, cols], 1.0, None, ALU.add)
                    else:
                        then_wait(dve.tensor_copy(gate[:, :], mod_ps[:, cols]))
                        then_wait(dve.scalar_tensor_tensor(gate_abs[:, :], gate[:, :], -1.0, gate[:, :],
                                                           ALU.mult, ALU.max))
                        then_wait(dve.tensor_scalar(gate_abs[:, :], gate_abs[:, :], 0.25, None, ALU.max))
                        then_wait(dve.tensor_scalar(gate_sign[:, :], mod_ps[:, cols], 0.0, 2.0,
                                                    ALU.is_ge, ALU.mult))
                        then_wait(dve.scalar_tensor_tensor(modrow[:, cols], gate_sign[:, :], -1.0,
                                                           gate_abs[:, :], ALU.add, ALU.mult))


def stage_projection(nc, a, dram, modrow, ident, scal, x_sb, lattice):
    with ExitStack() as ctx:
        sb = lambda n, s, dt=F32: ctx.enter_context(nc.sbuf_tensor(n, s, dt))
        ps = lambda n, s: ctx.enter_context(nc.psum_tensor(n, s, F32))
        sem = lambda n: ctx.enter_context(nc.semaphore(n))
        wqkv = sb("wqkv", [P, KC, 3 * D])
        wcode = sb("wcode", [P, KC, HROWS])
        head_sum = sb("head_sum", [H * HEX, H])
        soft_sum = sb("soft_sum", [HROWS, H])
        xm = sb("xm", [P, D])
        h = sb("h", [P, TPB, D])
        h_t = sb("h_t", [P, KC, BLK])
        qk_hi = sb("qk_hi", [P, 4, BLK], F32R)
        qk_lo = sb("qk_lo", [P, 4, BLK], F32R)
        code = sb("code", [HROWS, BLK])
        w_hi = sb("w_hi", [HROWS, BLK], F32R)
        w_lo = sb("w_lo", [HROWS, BLK], F32R)
        soft = sb("soft", [HROWS, BLK])
        s_hi = sb("s_hi", [HROWS, BLK], F32R)
        s_lo = sb("s_lo", [HROWS, BLK], F32R)
        soft_abs = sb("soft_abs", [HROWS, BLK])
        l_hi = sb("l_hi", [H * HEX, BLK], F32R)
        l_lo = sb("l_lo", [H * HEX, BLK], F32R)
        lat_abs = sb("lat_abs", [H * HEX, BLK])
        guard = sb("guard", [H, BLK])
        g_hi = sb("g_hi", [H, BLK], F32R)
        g_lo = sb("g_lo", [H, BLK], F32R)
        v_st = sb("v_st", [P, TPB, H, VW])
        tv_ps = ps("tv_ps", [P, 2 * BLK])
        qk_ps = ps("qk_ps", [P, 4 * BLK])
        code_ps = ps("code_ps", [P, BLK])
        lat_ps = ps("lat_ps", [P, BLK])

        w_in, waited = sem("pw_in"), sem("p_waited")
        norm_step, h_ready, transposed, h_t_ready = (
            sem("norm_step"), sem("h_ready"), sem("transposed"), sem("h_t_ready"))
        code_mm, qk_mm, lat_mm, v_mm, guard_mm = (
            sem("code_mm"), sem("qk_mm"), sem("lat_mm"), sem("v_mm"), sem("guard_mm"))
        code_ready, hi_ready, lo_ready, v_ready, lat_act, soft_ready, soft_abs_ready = (
            sem("code_ready"), sem("hi_ready"), sem("lo_ready"), sem("v_ready"), sem("lat_act"),
            sem("soft_ready"), sem("soft_abs_ready"))
        w_ready, s_ready, lat_ready, guard_step, g_ready = (
            sem("w_ready"), sem("s_ready"), sem("lat_ready"), sem("guard_step"), sem("g_ready"))
        st_qk = [sem(f"st_qk{m}") for m in range(4)]
        st_w, st_s, st_l, st_g, st_v = sem("st_w"), sem("st_s"), sem("st_l"), sem("st_g"), sem("st_v")
        block = ctx.enter_context(nc.Block())

        N_QK, N_W, N_S, N_L, N_G, N_V = 2, 4, 4, 4, 2, 1
        ST_0, TRANS_0, LO_0, LAT_0, V_0, GUARD_0, GMM_0, SABS_0, H_0 = 16, TPB, 4, 1, 1, 2, 1, 1, 1

        def part_rows(name, sides, parts, n, side, part, b, c):
            view = dram[name].rearrange("(z h q r) t -> z h q r t", h=sides, q=parts, r=n)
            return view[ds(b, 1), side, part, :, ds(c * BLK, BLK)].rearrange("z h r t -> (z h) r t")

        @block.sync
        def _(sp):
            for s in st_qk + [st_w, st_s, st_l, st_g, st_v]:
                sp.sem_inc(s, ST_0)
            sp.dma_start(wcode[:, :, :], a["code_wt"].rearrange("(k p) n -> p k n", p=P)).then_inc(w_in, 16)
            sp.dma_start(wqkv[:, :, :], a["qkv_wt"].rearrange("(k p) n -> p k n", p=P)).then_inc(w_in, 16)
            sp.dma_start(head_sum[:, :], a["head_sum"]).then_inc(w_in, 16)
            sp.dma_start(soft_sum[:, :], a["soft_sum"]).then_inc(w_in, 16)
            with sp.Fori(0, B) as b, sp.Fori(0, NBLK) as c:
                i = b * NBLK + c
                cols = ds(c * BLK, BLK)
                sp.wait_ge(w_ready, i * 2 + 2)
                for part in range(4):
                    sp.dma_start(part_rows("code_split", 2, 4, HEX, slice(0, 2), part, b, c),
                                 (w_hi, w_lo, w_lo, w_hi)[part][:, :].bitcast(F32)).then_inc(st_w, 16)
                sp.wait_ge(s_ready, i * 2 + 2)
                for part in range(4):
                    sp.dma_start(part_rows("soft_split", 1, 4, HEX, slice(0, 1), part, b, c),
                                 (s_hi, s_lo)[part % 2][HEX:HROWS, :].bitcast(F32)).then_inc(st_s, 16)
                for m in range(4):
                    sp.wait_ge(lo_ready, i * 4 + (LO_0 + m + 1))
                    sp.sem_inc(waited, 1)
                    for part, src in enumerate((qk_hi, qk_lo)):
                        sp.dma_start(part_rows("q_split" if m < 2 else "k_split", H, 2, HD,
                                               slice((m % 2) * 8, (m % 2) * 8 + 8), part, b, c),
                                     src[:, m, :].bitcast(F32)).then_inc(st_qk[m], 16)
                sp.wait_ge(lat_ready, i + (LAT_0 + 1))
                for part in range(4):
                    sp.dma_start(part_rows("lat_split", H, 4, HEX, slice(0, H), part, b, c),
                                 (l_hi, l_lo)[part % 2][:, :].bitcast(F32)).then_inc(st_l, 16)
                sp.wait_ge(v_ready, i + (V_0 + 1))
                sp.dma_start(dram["v_rows"][ds(i * BLK, BLK), :].rearrange("(n p) v -> p n v", p=P),
                             v_st[:, :, :, :].rearrange("p t h v -> p t (h v)")).then_inc(st_v, 16)
                sp.wait_ge(g_ready, i + 1)
                for part, src in enumerate((g_hi, g_lo)):
                    dst = part_rows("guard_split", H, 2, 1, slice(0, H), part, b, c)
                    sp.dma_start(dst.rearrange("h r t -> (h r) t"), src[:, :].bitcast(F32)).then_inc(st_g, 16)
            for s, n in [(s, N_QK) for s in st_qk] + [
                    (st_w, N_W), (st_s, N_S), (st_l, N_L), (st_g, N_G), (st_v, N_V)]:
                sp.wait_ge(s, ST_0 + 16 * n * B * NBLK)

        @block.gpsimd
        def _(pool):
            pool.sem_inc(h_ready, H_0)
            with pool.Fori(0, B) as b, pool.Fori(0, NBLK) as c:
                for t in range(TPB):
                    tile = b * (NBLK * TPB) + c * TPB + t
                    pool.wait_ge(h_ready, tile + H_0)
                    pool.sem_inc(waited, 1)
                    pool.tensor_tensor(xm[:, :], x_sb[:, ds(tile * D, D)], modrow[:, ds(b * (6 * D) + D, D)],
                                       ALU.mult).then_inc(norm_step, 1)
                    pool.wait_ge(norm_step, tile + 1)
                    pool.wait_ge(transposed, tile + (TRANS_0 - TPB + 1))
                    pool.sem_inc(waited, 1)
                    pool.tensor_tensor(h[:, t, :], xm[:, :], modrow[:, ds(b * (6 * D), D)],
                                       ALU.add).then_inc(h_ready, 1)

        @block.tensor
        def _(pe):
            pe.sem_inc(transposed, TRANS_0)
            pe.sem_inc(guard_mm, GMM_0)
            pe.wait_ge(w_in, 64)
            with pe.Fori(0, B * NBLK) as i:
                pe.wait_ge(v_ready, i + V_0)
                for t in range(TPB):
                    pe.wait_ge(h_ready, i * TPB + (t + 1 + H_0))
                    for k in range(KC):
                        tr = pe.transpose(tv_ps[:, k * BLK + t * P:k * BLK + (t + 1) * P],
                                          h[:, t, k * P:(k + 1) * P], ident[:, :])
                    tr.then_inc(transposed, 1)
                pe.wait_ge(h_t_ready, i + 1)
                pe.wait_ge(guard_step, i * 2 + (GUARD_0 - 1))
                for k in range(KC):
                    mm = pe.matmul(code_ps[0:HROWS, :], wcode[:, k, :], h_t[:, k, :],
                                   start=(k == 0), stop=(k == KC - 1))
                mm.then_inc(code_mm, 1)
                for m in range(4):
                    pe.wait_ge(lo_ready, i * 4 + (m + 1))
                    for k in range(KC):
                        mm = pe.matmul(qk_ps[:, m * BLK:(m + 1) * BLK], wqkv[:, k, m * P:(m + 1) * P],
                                       h_t[:, k, :], start=(k == 0), stop=(k == KC - 1))
                    mm.then_inc(qk_mm, 1)
                pe.wait_ge(code_ready, i + 1)
                pe.wait_ge(lat_ready, i + LAT_0)
                pe.matmul(lat_ps[0:H * HEX, :], lattice[:, :], code[0:HEX, :],
                          start=True, stop=True).then_inc(lat_mm, 1)
                for t in range(TPB):
                    for k in range(KC):
                        mm = pe.matmul(tv_ps[:, t * D:(t + 1) * D], h_t[:, k, t * P:(t + 1) * P],
                                       wqkv[:, k, 2 * D:3 * D], start=(k == 0), stop=(k == KC - 1))
                mm.then_inc(v_mm, 1)
                pe.wait_ge(lat_act, i + 1)
                pe.wait_ge(soft_abs_ready, i + (SABS_0 + 1))
                pe.matmul(code_ps[0:H, :], head_sum[:, :], lat_abs[:, :], start=True, stop=False)
                pe.matmul(code_ps[0:H, :], soft_sum[:, :], soft_abs[:, :], start=False, stop=True
                          ).then_inc(guard_mm, 1)

        @block.scalar
        def _(act):
            act.sem_inc(soft_abs_ready, SABS_0)
            with act.Fori(0, B * NBLK) as i:
                act.wait_ge(transposed, i * TPB + (TRANS_0 + TPB))
                act.activation(h_t[:, :, :], tv_ps[:, :].rearrange("p (k t) -> p k t", k=KC),
                               ACT.Copy).then_inc(h_t_ready, 1)
                act.wait_ge(code_mm, i + 1)
                act.activation(code[:, :], code_ps[0:HROWS, :], ACT.Tanh).then_inc(code_ready, 1)
                for m in range(4):
                    act.wait_ge(qk_mm, i * 4 + (m + 1))
                    act.wait_ge(st_qk[m], i * (16 * N_QK) + ST_0)
                    act.activation(qk_hi[:, m, :], qk_ps[:, m * BLK:(m + 1) * BLK], ACT.Copy,
                                   scale=scal[:, INV_BETA:INV_BETA + 1] if m < 2 else 1.0
                                   ).then_inc(hi_ready, 1)
                act.wait_ge(soft_ready, i + 1)
                act.wait_ge(guard_mm, i + GMM_0)
                act.activation(soft_abs[:, :], soft[:, :], ACT.Abs).then_inc(soft_abs_ready, 1)
                act.wait_ge(lat_mm, i + 1)
                act.activation(lat_abs[:, :], lat_ps[0:H * HEX, :], ACT.Abs)
                act.wait_ge(st_l, i * (16 * N_L) + ST_0)
                act.activation(l_hi[:, :], lat_ps[0:H * HEX, :], ACT.Copy).then_inc(lat_act, 1)

        @block.vector
        def _(dve):
            dve.sem_inc(lo_ready, LO_0)
            dve.sem_inc(lat_ready, LAT_0)
            dve.sem_inc(guard_step, GUARD_0)
            dve.memset(v_st[:, :, :, HD:VW], 1.0).then_inc(v_ready, V_0)
            with dve.Fori(0, B * NBLK) as i:
                dve.wait_ge(code_ready, i + 1)
                dve.wait_ge(st_w, i * (16 * N_W) + ST_0)
                dve.tensor_copy(w_hi[:, :], code[:, :]).then_inc(w_ready, 1)
                dve.wait_ge(soft_abs_ready, i + SABS_0)
                dve.tensor_scalar(soft[:, :], code[:, :], scal[0:HROWS, HALF_LAM:HALF_LAM + 1], None,
                                  ALU.mult).then_inc(soft_ready, 1)
                dve.wait_ge(w_ready, i * 2 + 1)
                dve.tensor_tensor(w_lo[:, :], code[:, :], w_hi[:, :].bitcast(F32), ALU.subtract
                                  ).then_inc(w_ready, 1)
                dve.wait_ge(soft_ready, i + 1)
                dve.wait_ge(st_s, i * (16 * N_S) + ST_0)
                dve.tensor_copy(s_hi[:, :], soft[:, :]).then_inc(s_ready, 1)
                dve.wait_ge(s_ready, i * 2 + 1)
                dve.tensor_tensor(s_lo[:, :], soft[:, :], s_hi[:, :].bitcast(F32), ALU.subtract
                                  ).then_inc(s_ready, 1)
                for m in range(4):
                    dve.wait_ge(hi_ready, i * 4 + (m + 1))
                    dve.scalar_tensor_tensor(qk_lo[:, m, :], qk_ps[:, m * BLK:(m + 1) * BLK],
                                             scal[:, INV_BETA:INV_BETA + 1] if m < 2 else 1.0,
                                             qk_hi[:, m, :].bitcast(F32), ALU.mult, ALU.subtract
                                             ).then_inc(lo_ready, 1)
                dve.wait_ge(lat_act, i + 1)
                dve.tensor_tensor(l_lo[:, :], lat_ps[0:H * HEX, :], l_hi[:, :].bitcast(F32), ALU.subtract
                                  ).then_inc(lat_ready, 1)
                dve.wait_ge(v_mm, i + 1)
                dve.wait_ge(st_v, i * (16 * N_V) + ST_0)
                dve.tensor_copy(v_st[:, :, :, 0:HD],
                                tv_ps[:, :].rearrange("p (t h d) -> p t h d", t=TPB, h=H)).then_inc(v_ready, 1)
                dve.wait_ge(guard_mm, i + (GMM_0 + 1))
                dve.tensor_scalar(guard[:, :], code_ps[0:H, :], -1.0, scal[0:H, ROOM:ROOM + 1],
                                  ALU.mult, ALU.add).then_inc(guard_step, 1)
                dve.wait_ge(guard_step, i * 2 + (GUARD_0 + 1))
                dve.wait_ge(st_g, i * (16 * N_G) + ST_0)
                dve.tensor_scalar(g_hi[:, :], guard[:, :], 0.0, None, ALU.min).then_inc(guard_step, 1)
                dve.wait_ge(guard_step, i * 2 + (GUARD_0 + 2))
                dve.scalar_tensor_tensor(g_lo[:, :], guard[:, :], 0.0, g_hi[:, :].bitcast(F32),
                                         ALU.min, ALU.subtract).then_inc(g_ready, 1)


def stage_attention(nc, a, dram, scal, rows_sb, x_back):
    with ExitStack() as ctx:
        sb = lambda n, s, dt=F32: ctx.enter_context(nc.sbuf_tensor(n, s, dt))
        ps = lambda n, s: ctx.enter_context(nc.psum_tensor(n, s, F32))
        sem = lambda n: ctx.enter_context(nc.semaphore(n))
        k_st = sb("k_st", [P, HG // 2, T], F32R)
        q_mv = sb("q_mv", [P, HG, T], F32R)
        w_st = sb("w_st", [P, T], F32R)
        u_mv = sb("u_mv", [P, HG, T], F32R)
        v_sb = sb("v_sb", [P, T // P, HG * VW])
        probs = sb("probs", [P, NBUF, HG, BLK])
        o_sb = sb("o_sb", [P, 2, BLK])
        raw_ps = ps("raw_ps", [P, HG, BLK])
        bil_ps = ps("bil_ps", [P, 2, BLK])
        o_ps = ps("o_ps", [P, BLK])
        pad_ready, zeroed, waited = sem("pad_ready"), sem("zeroed"), sem("a_waited")
        waited_sp = sem("a_waited_sp")
        loaded = [sem(f"loaded{c}") for c in range(NBLK)]
        raw_mm, bil_mm, pv_mm = sem("raw_mm"), sem("bil_mm"), sem("pv_mm")
        tanh_ready, sum_ready, exp_ready, mask_ready = (
            sem("tanh_ready"), sem("sum_ready"), sem("exp_ready2"), sem("mask_ready"))
        o_ready = sem("o_ready")
        o_stored = [sem(f"o_stored{p}") for p in range(2)]
        block = ctx.enter_context(nc.Block())

        N_LOADS = 6 + 4 + 3 + 1 + 1
        PV_0, TANH_0, SUM_0, O_0, ST_0 = NSTEP, 1, 2, 1, 16

        def load_block(sp, it, c):
            cols = slice(c * BLK, (c + 1) * BLK)
            load = lambda dst, src: sp.dma_start(dst.bitcast(F32), src).then_inc(loaded[c], 16)
            heads = lambda name, n: dram[name][ds(it * (HG * n), HG * n), cols]
            k_rows = heads("k_split", 2 * HD).rearrange("(j z s r) t -> z s r j t", z=2, s=2, r=HD)
            q_rows = heads("q_split", 2 * HD).rearrange("(j z r) t -> z r j t", z=2, r=2 * HD)
            k_both = heads("k_split", 2 * HD).rearrange("(j z r) t -> z r j t", z=2, r=2 * HD)
            sp.wait_ge(pv_mm, it * NSTEP + (PV_0 - NSTEP + LAST_USE[c] + 1))
            sp.sem_inc(waited_sp, 1)
            for z in range(2):
                row = z * ROWS
                load(k_st[row:row + 2 * HD, :, cols], k_both[z])
                load(k_st[row + 2 * HD:row + 3 * HD, :, cols], k_rows[z, 1])
                load(k_st[row + 3 * HD:row + 4 * HD, :, cols], k_rows[z, 0])
                for half in range(2):
                    load(q_mv[row + half * 2 * HD:row + (half + 1) * 2 * HD, z::2, cols], q_rows[z])
            n = 4 * HEX
            load(u_mv[0:n, :, cols], heads("lat_split", n).rearrange("(j r) t -> r j t", r=n))
            soft = dram["soft_split"][ds(it // NG * n, n), cols]
            load(u_mv[n:2 * n, :, cols], soft.rearrange("r (o t) -> r o t", o=1).broadcast_to([n, HG, BLK]))
            load(u_mv[2 * n:BIAS_ROWS, :, cols], heads("guard_split", 2).rearrange("(j r) t -> r j t", r=2))
            load(w_st[0:2 * n, cols], dram["code_split"][ds(it // NG * (2 * n), 2 * n), cols])
            sp.dma_start(v_sb[:, c * TPB:(c + 1) * TPB, :],
                         dram["v_rows"][ds(it // NG * T + c * BLK, BLK), ds(it % NG * (HG * VW), HG * VW)
                                        ].rearrange("(n p) v -> p n v", p=P)
                         ).then_inc(loaded[c], 16)

        def store_out(sp, it, qb):
            sp.wait_ge(o_ready, it * NBLK + (O_0 + qb + 1))
            sp.dma_start(dram["o_t"][ds(it * P, P), qb * BLK:(qb + 1) * BLK],
                         o_sb[:, qb % 2, :]).then_inc(o_stored[qb % 2], 16)

        @block.sync
        def _(sp):
            for s in o_stored:
                sp.sem_inc(s, ST_0)
            sp.wait_ge(pad_ready, 2)
            for c in range(NBLK):
                sp.wait_ge(zeroed, 2 * (c + 1))
                load_block(sp, 0, c)
            sp.dma_start(rows_sb[:, :].rearrange("p (n d) -> p n d", d=PAY)[:, :, 0:D],
                         a["x"].rearrange("(n p) d -> p n d", p=P)).then_inc(x_back, 16)

            def iteration(it, last):
                for qb in range(NBLK):
                    if qb == NBLK - 1 and not last:
                        for c in range(NBLK):
                            load_block(sp, it + 1, c)
                    store_out(sp, it, qb)

            with sp.Fori(0, NIT - 1) as it:
                iteration(it, False)
            iteration(NIT - 1, True)
            for s in o_stored:
                sp.wait_ge(s, ST_0 + 16 * NIT * NBLK // 2)

        @block.gpsimd
        def _(pool):
            for c in range(NBLK):
                for mv in (q_mv, u_mv):
                    pool.memset(mv[:, :, c * BLK:(c + 1) * BLK].bitcast(U32), 0).then_inc(zeroed, 1)
            with pool.Fori(0, NIT) as it:
                for s in DIAG:
                    pool.wait_ge(exp_ready, it * NSTEP + (s + 1))
                    pool.sem_inc(waited, 1)
                    for _, column, _, _ in STEPS[s][1]:
                        tri = probs[:, s % NBUF, :, column:column + P]
                        mask = pool.affine_select(out=tri, in_=tri, compare_op=ALU.is_ge, fill=0.0, base=0,
                                                  pattern=[[0, HG], [1, P]], channel_multiplier=-1)
                    mask.then_inc(mask_ready, 1)

        @block.tensor
        def _(pe):
            pe.sem_inc(pv_mm, PV_0)

            def raw_scores(it, s):
                qb, pieces = STEPS[s]
                if s == FIRST_OF[qb]:
                    pe.wait_ge(loaded[qb], it * (16 * N_LOADS) + 16 * N_LOADS)
                pe.wait_ge(tanh_ready, it * NSTEP + (s + TANH_0))
                for kt, column, query, width in pieces:
                    for hd in range(HG):
                        mm = pe.matmul(raw_ps[:, hd, column:column + width],
                                       k_st[:, hd // 2, kt * P:(kt + 1) * P],
                                       q_mv[:, hd, qb * BLK + query:qb * BLK + query + width],
                                       start=True, stop=True)
                mm.then_inc(raw_mm, 1)

            def bilinear(it, s, heads):
                qb, pieces = STEPS[s]
                for hd in heads:
                    pe.wait_ge(sum_ready, it * (HG * NSTEP) + (HG * s + hd - 1 + SUM_0))
                    for kt, column, query, width in pieces:
                        mm = pe.matmul(bil_ps[:, hd % 2, column:column + width], w_st[:, kt * P:(kt + 1) * P],
                                       u_mv[:, hd, qb * BLK + query:qb * BLK + query + width],
                                       start=True, stop=True)
                    mm.then_inc(bil_mm, 1)

            def weighted_values(it, s):
                qb, pieces = STEPS[s]
                if s in DIAG:
                    pe.wait_ge(mask_ready, it * len(DIAG) + (DIAG.index(s) + 1))
                else:
                    pe.wait_ge(exp_ready, it * NSTEP + (s + 1))
                if s == FIRST_OF[qb]:
                    pe.wait_ge(o_ready, it * NBLK + (qb + O_0))
                for kt, column, query, width in pieces:
                    for hd in range(HG):
                        mm = pe.matmul(o_ps[hd * VW:(hd + 1) * VW, query:query + width],
                                       v_sb[:, kt, hd * VW:(hd + 1) * VW],
                                       probs[:, s % NBUF, hd, column:column + width],
                                       start=(s == FIRST_OF[qb]), stop=(s == LAST_OF[qb]))
                mm.then_inc(pv_mm, 1)

            FIRST_TWO, LAST_TWO = (0, 1), (2, 3)
            for s in range(PE_LEAD):
                raw_scores(0, s)
                if s:
                    bilinear(0, s - 1, LAST_TWO)
                bilinear(0, s, FIRST_TWO)

            def iteration(it, last):
                for s in range(NSTEP):
                    at = lambda n: (it, n) if n < NSTEP else None if last else (it + 1, n - NSTEP)
                    if at(s + PE_LEAD):
                        raw_scores(*at(s + PE_LEAD))
                    if at(s + PE_LEAD - 1):
                        bilinear(*at(s + PE_LEAD - 1), LAST_TWO)
                    weighted_values(it, s)
                    if at(s + PE_LEAD):
                        bilinear(*at(s + PE_LEAD), FIRST_TWO)

            with pe.Fori(0, NIT - 1) as it:
                iteration(it, False)
            iteration(NIT - 1, True)

        @block.scalar
        def _(act):
            act.sem_inc(tanh_ready, TANH_0)

            def tanh(it, s):
                first = first_column(s)
                act.wait_ge(raw_mm, it * NSTEP + (s + 1))
                act.wait_ge(pv_mm, it * NSTEP + (PV_0 + s + 1 - NBUF))
                act.activation(probs[:, s % NBUF, :, first:BLK], raw_ps[:, :, first:BLK], ACT.Tanh
                               ).then_inc(tanh_ready, 1)

            def exp(it, s):
                first = first_column(s)
                act.wait_ge(sum_ready, it * (HG * NSTEP) + (HG * (s + 1) + SUM_0))
                scores = probs[:, s % NBUF, :, first:BLK]
                act.activation(scores, scores, ACT.Exp).then_inc(exp_ready, 1)

            tanh(0, 0)

            def iteration(it, last):
                for s in range(NSTEP):
                    if s + 1 < NSTEP:
                        tanh(it, s + 1)
                    elif not last:
                        tanh(it + 1, 0)
                    exp(it, s)

            with act.Fori(0, NIT - 1) as it:
                iteration(it, False)
            iteration(NIT - 1, True)

        @block.vector
        def _(dve):
            dve.memset(w_st[0:ROWS, :].bitcast(F32), 1.0).then_inc(pad_ready, 1)
            dve.memset(w_st[ROWS:P, :].bitcast(F32), 0.0).then_inc(pad_ready, 1)
            dve.sem_inc(sum_ready, SUM_0)
            dve.sem_inc(o_ready, O_0)

            def score_sums(it, s):
                first = first_column(s)
                dve.wait_ge(tanh_ready, it * NSTEP + (s + 1 + TANH_0))
                for hd in range(HG):
                    dve.wait_ge(bil_mm, it * (HG * NSTEP) + (HG * s + hd + 1))
                    scores = probs[:, s % NBUF, hd, first:BLK]
                    dve.scalar_tensor_tensor(scores, scores, scal[:, ALPHA:ALPHA + 1],
                                             bil_ps[:, hd % 2, first:BLK], ALU.mult, ALU.add
                                             ).then_inc(sum_ready, 1)

            def evacuate(it, qb):
                dve.wait_ge(pv_mm, it * NSTEP + (PV_0 + LAST_OF[qb] + 1))
                dve.wait_ge(o_stored[qb % 2], it * (16 * NBLK // 2) + (16 * (qb // 2) + ST_0))
                dve.tensor_copy(o_sb[:, qb % 2, :], o_ps[:, :]).then_inc(o_ready, 1)

            for s in range(DVE_LEAD):
                score_sums(0, s)

            def iteration(it, last):
                for s in range(NSTEP):
                    ahead = s + DVE_LEAD
                    if ahead < NSTEP:
                        score_sums(it, ahead)
                    elif not last:
                        score_sums(it + 1, ahead - NSTEP)
                    if s == LAST_OF[STEPS[s][0]]:
                        evacuate(it, STEPS[s][0])

            with dve.Fori(0, NIT - 1) as it:
                iteration(it, False)
            iteration(NIT - 1, True)


def skewed(eng, total, lag, unroll, emit):
    peeled = -(-lag // unroll) * unroll
    for m in range(peeled):
        emit(m, m, lambda k: 0 <= m - k < total)
    with eng.Fori(peeled // unroll, total // unroll) as i:
        for u in range(unroll):
            emit(i * unroll + u, u, lambda k: True)
    for m in range(total, total + lag):
        emit(m, m, lambda k: 0 <= m - k < total)


def stage_output(nc, a, dram, modrow, ident, rows_sb, stats2, rstd2, token_f, blank, out, rw1, router_weights,
                 pad_base, tile_first, x_back):
    with ExitStack() as ctx:
        sb = lambda n, s, dt=F32: ctx.enter_context(nc.sbuf_tensor(n, s, dt))
        ps = lambda n, s: ctx.enter_context(nc.psum_tensor(n, s, F32))
        sem = lambda n: ctx.enter_context(nc.semaphore(n))
        OB = 4
        wo = sb("wo", [P, KC, D])
        o_t = sb("o_t_sb", [P, OB, NG, P])
        rden = sb("rden", [P, H])
        attn = sb("attn", [P, 2, D])
        attn_t = sb("attn_t", [P, 2, D])
        gated = sb("gated", [P, D])
        bn = sb("bn2", [P, NTILE * 6])
        o_tr_ps = ps("o_tr_ps", [P, 2, BLK])
        a_tr_ps = ps("a_tr_ps", [P, 2, BLK])
        proj_ps = ps("proj_ps", [P, 2, BLK])
        waited = sem("o_waited")
        rw_in, rw2_zeroed, rw1_split = sem("rw_in"), sem("rw2_zeroed"), sem("rw1_split")
        rw1_hi, rw1_lo, rw2, rb1, rb2, before, all_ones, expert_iota, region_base = router_weights
        w_in, t_in, blank_ready, blank_stored = sem("wo_in"), sem("t_in"), sem("blank_ready"), sem("blank_stored")
        o_in = [sem(f"o_in{p}") for p in range(OB)]
        o_tr_mm, a_tr_mm, proj_mm = sem("o_tr_mm"), sem("a_tr_mm"), sem("proj_mm")
        rden_ready, attn_ready, attn_t_ready, gated_ready, x1_ready, stats_ready, var_ready, std_ready = (
            sem("rden_ready"), sem("attn_ready"), sem("attn_t_ready"), sem("gated_ready"), sem("x1_ready"),
            sem("stats_ready"), sem("var_ready2"), sem("std_ready2"))
        block = ctx.enter_context(nc.Block())
        OTR_0, ATTN_0, ATR_0, ATT_0, PROJ_0, GATED_0, X1_0 = OB, 2, 2, 2, 2, 2, 1

        @block.sync
        def _(sp):
            ov = dram["o_t"].rearrange("(z g p) t -> z p g t", g=NG, p=P)

            def load(m, u, active):
                if active(0):
                    sp.wait_ge(o_tr_mm, m + (OTR_0 - OB + 1))
                    sp.sem_inc(waited, 1)
                    src = ov[ds(m // (NBLK * TPB), 1), :, :, ds(m % (NBLK * TPB) * P, P)]
                    sp.dma_start(o_t[:, u % OB, :, :], src.rearrange("z p g t -> (z p) g t")
                                 ).then_inc(o_in[u % OB], 16)

            sp.dma_start(wo[:, :, :], a["out_wt"].rearrange("(k p) n -> p k n", p=P)).then_inc(w_in, 16)
            sp.dma_start(token_f[:, :], a["token_rows"]).then_inc(t_in, 16)
            for m in range(OB):
                load(m, m, lambda k: True)
            sp.dma_start(rw1[:, :].rearrange("p (k n) -> p k n", k=KC),
                         a["rw1"].rearrange("(k p) n -> p k n", p=P)).then_inc(rw_in, 16)
            sp.dma_start(rb1[:, :], a["rb1_cols"]).then_inc(rw_in, 16)
            sp.dma_start(rb2[:, :], a["rb2"].partition_broadcast(P)).then_inc(rw_in, 16)
            sp.dma_start(before[:, :], a["before"]).then_inc(rw_in, 16)
            sp.dma_start(all_ones[:, :], a["ones"]).then_inc(rw_in, 16)
            sp.dma_start(expert_iota[:, :], a["iota"][0:E].partition_broadcast(P)).then_inc(rw_in, 16)
            sp.dma_start(region_base[:, :], a["region_base"].partition_broadcast(P)).then_inc(rw_in, 16)
            sp.wait_ge(rw2_zeroed, 1)
            sp.dma_start(rw2[:, :, 0:E], a["rw2"].rearrange("(c p) e -> p c e", p=P)).then_inc(rw_in, 16)
            sp.dma_start(pad_base[:, :], a["pad_base"]).then_inc(rw_in, 16)
            sp.dma_start(tile_first[:, :], a["iota"].partition_broadcast(P)).then_inc(rw_in, 16)
            with sp.Fori(1, NTILE // OB) as i:
                for u in range(OB):
                    load(i * OB + u, u, lambda k: True)
            sp.wait_ge(rw_in, 160)
            sp.wait_ge(blank_ready, 2)
            sp.dma_start(dram["x_rows"][VOID:VOID + P, :], blank[:, :]).then_inc(blank_stored, 16)
            sp.dma_start(out[NTOK:NTOK + P, :], blank[:, 0:D]).then_inc(blank_stored, 16)
            sp.wait_ge(blank_stored, 32)

        @block.tensor
        def _(pe):
            pe.sem_inc(o_tr_mm, OTR_0)
            pe.sem_inc(proj_mm, PROJ_0)
            pe.sem_inc(a_tr_mm, ATR_0)
            pe.wait_ge(w_in, 16)

            def step(m, u, active):
                if active(0):
                    pe.wait_ge(o_in[u % OB], (m // OB) * 16 + 16)
                    pe.wait_ge(attn_ready, m + (ATTN_0 - 1))
                    for g in range(NG):
                        tr = pe.transpose(o_tr_ps[:, u % 2, g * P:(g + 1) * P], o_t[:, u % OB, g, :], ident[:, :])
                    tr.then_inc(o_tr_mm, 1)
                if active(1):
                    n, p = m - 1, (u - 1) % 2
                    pe.wait_ge(attn_ready, n + (ATTN_0 + 1))
                    pe.wait_ge(attn_t_ready, n + (ATT_0 - 1))
                    for k in range(KC):
                        tr = pe.transpose(a_tr_ps[:, p, k * P:(k + 1) * P], attn[:, p, k * P:(k + 1) * P],
                                          ident[:, :])
                    tr.then_inc(a_tr_mm, 1)
                if active(2):
                    n, p = m - 2, u % 2
                    pe.wait_ge(attn_t_ready, n + (ATT_0 + 1))
                    pe.wait_ge(gated_ready, n + (GATED_0 - 1))
                    for k in range(KC):
                        mm = pe.matmul(proj_ps[:, p, 0:D], attn_t[:, p, k * P:(k + 1) * P], wo[:, k, :],
                                       start=(k == 0), stop=(k == KC - 1))
                    mm.then_inc(proj_mm, 1)

            skewed(pe, NTILE, 2, OB, step)

        @block.scalar
        def _(act):
            act.sem_inc(attn_t_ready, ATT_0)
            with act.Fori(0, NTILE // 2) as i:
                for p in range(2):
                    n = i * 2 + p
                    act.wait_ge(a_tr_mm, n + (ATR_0 + 1))
                    act.wait_ge(proj_mm, n + (PROJ_0 - 1))
                    act.activation(attn_t[:, p, :], a_tr_ps[:, p, 0:D], ACT.Copy).then_inc(attn_t_ready, 1)
            act.wait_ge(var_ready, 1)
            act.activation(rstd2[:, :], rstd2[:, :], ACT.Sqrt).then_inc(std_ready, 1)

        @block.gpsimd
        def _(pool):
            pool.sem_inc(x1_ready, X1_0)
            pool.memset(rw2[:, :, :], 0.0).then_inc(rw2_zeroed, 1)
            pool.wait_ge(rw_in, 160)
            pool.tensor_copy(rw1_hi[:, :], rw1[:, :]).then_inc(rw1_split, 1)
            pool.wait_ge(rw1_split, 1)
            pool.tensor_tensor(rw1_lo[:, :], rw1[:, :], rw1_hi[:, :].bitcast(F32), ALU.subtract)
            pool.wait_ge(x_back, 16)
            with pool.Fori(0, NTILE) as n:
                pool.wait_ge(gated_ready, n + (GATED_0 + 1))
                x1 = rows_sb[:, ds(n * PAY, D)]
                pool.tensor_tensor(x1, x1, gated[:, :], ALU.add).then_inc(x1_ready, 1)

        @block.vector
        def _(dve):
            dve.sem_inc(attn_ready, ATTN_0)
            dve.sem_inc(gated_ready, GATED_0)
            dve.memset(blank[:, :], 0.0).then_inc(blank_ready, 1)
            dve.wait_ge(x_back, 16)
            dve.wait_ge(t_in, 16)
            dve.wait_ge(blank_ready, 1)
            dve.tensor_copy(blank[:, TOKEN:PAY], token_f[:, NTILE:NTILE + 1]).then_inc(blank_ready, 1)

            def step(m, u, active):
                if active(0):
                    heads = o_tr_ps[:, u % 2, :].rearrange("p (h v) -> p h v", v=VW)
                    dve.wait_ge(o_tr_mm, m + (OTR_0 + 1))
                    dve.wait_ge(a_tr_mm, m + (ATR_0 - 1))
                    dve.wait_ge(attn_ready, m + ATTN_0)
                    dve.reciprocal(rden[:, :], heads[:, :, HD]).then_inc(rden_ready, 1)
                    dve.wait_ge(rden_ready, m + 1)
                    dve.tensor_tensor(attn[:, u % 2, :].rearrange("p (h d) -> p h d", d=HD), heads[:, :, 0:HD],
                                      rden[:, :].rearrange("p (h o) -> p h o", o=1).broadcast_to([P, H, HD]),
                                      ALU.mult).then_inc(attn_ready, 1)
                if active(2):
                    n = m - 2
                    dve.wait_ge(proj_mm, n + (PROJ_0 + 1))
                    dve.wait_ge(x1_ready, n + X1_0)
                    gate = modrow[:, ds(n // (NBLK * TPB) * (6 * D) + 2 * D, D)]
                    dve.tensor_tensor(gated[:, :], proj_ps[:, u % 2, 0:D], gate, ALU.mult).then_inc(gated_ready, 1)
                if active(3):
                    n = m - 3
                    dve.wait_ge(x1_ready, n + (X1_0 + 1))
                    dve.bn_stats(bn[:, ds(n * 6, 6)], rows_sb[:, ds(n * PAY, D)]).then_inc(stats_ready, 1)

            skewed(dve, NTILE, 3, 2, step)
            dve.wait_ge(stats_ready, NTILE)
            for n in range(NTILE):
                last = dve.bn_aggr(stats2[:, 2 * n:2 * n + 2], bn[:, 6 * n:6 * n + 6])
            last.then_inc(stats_ready, 1)
            dve.wait_ge(stats_ready, NTILE + 1)
            pairs = stats2[:, :].rearrange("p (n s) -> p n s", s=2)
            dve.tensor_scalar(rstd2[:, :], pairs[:, :, 1], EPS, None, ALU.add).then_inc(var_ready, 1)
            dve.wait_ge(std_ready, 1)
            dve.reciprocal(rstd2[:, :], rstd2[:, :]).then_inc(var_ready, 1)
            dve.wait_ge(var_ready, 2)
            dve.scalar_tensor_tensor(pairs[:, :, 0], pairs[:, :, 0], -1.0, rstd2[:, :], ALU.mult, ALU.mult)


def stage_router(nc, a, dram, modrow, ident, rows_sb, stats2, rstd2, token_f, blank, w1, w1_in, out,
                 router_weights, pad_base, tile_first, tile_expert, expert_f, tile_row, pad_row):
    with ExitStack() as ctx:
        sb = lambda n, s, dt=F32: ctx.enter_context(nc.sbuf_tensor(n, s, dt))
        ps = lambda n, s: ctx.enter_context(nc.psum_tensor(n, s, F32))
        sem = lambda n: ctx.enter_context(nc.semaphore(n))
        HC = HID // P
        SLOTS = TPB * TOPK
        rw1_hi, rw1_lo, rw2, rb1, rb2, before, all_ones, expert_iota, region_base = router_weights
        xn = sb("xn2", [P, 2, D])
        h2_blk = sb("h2_blk", [P, 2, TPB, D])
        h2_hi = sb("h2_hi", [P, 2, KC, BLK], F32R)
        h2_lo = sb("h2_lo", [P, 2, KC, BLK], F32R)
        act_t = sb("act_t", [P, 2, HC, BLK])
        log_sb = sb("log_sb", [P, P])
        logits = sb("logits", [P, TPB, E])
        logit_diff = sb("logit_diff", [P, TPB])
        prob_diff = sb("prob_diff", [P, TPB])
        top8 = sb("top8", [P, TPB, E])
        index8 = sb("index8", [P, TPB, E], U32)
        index_f = sb("index_f", [P, TPB, TOPK])
        hot = sb("r_hot", [P, TPB, TOPK, E])
        both = sb("r_both", [P, TPB, E])
        seen = sb("seen", [P, TPB + 1, E])
        row = sb("r_row", [P, TPB, E])
        picked = sb("r_picked", [P, TPB, TOPK, E])
        place_f = sb("place_f", [P, SLOTS])
        place = sb("place", [P, NTILE * TOPK], U32)
        HB = 3
        tr_ps = ps("tr_ps", [P, KC, BLK])
        hid_ps = ps("hid_ps", [P, HB, BLK])
        log_ps = ps("log_ps", [P, BLK])
        lgt_ps = ps("lgt_ps", [P, BLK])
        rank_ps = ps("rank_ps", [P, BLK])
        count = sb("count", [P, E])
        count_i = sb("count_i", [P, E], U32)
        padded = sb("padded", [P, E])
        start = sb("start", [P, 2, E])
        passed = sb("passed", [P, NET, E])
        skipped = sb("skipped", [P, E])
        row_f = sb("row_f", [P, NET])
        waited = sem("r_waited")
        scattered, sums_mm, chain, pads_ready = (
            sem("scattered"), sem("sums_mm"), sem("dispatch_chain"), sem("pads_ready"))
        x1_stored, h2_kept = sem("x1_stored"), sem("h2_kept")
        ln_step, h2_ready, tr_mm, h2_t_step, hid_mm, act_ready, log_mm, log_ready, lgt_mm = (
            sem("ln_step"), sem("h2_ready"), sem("tr_mm"), sem("h2_t_step"), sem("hid_mm"), sem("act_ready"),
            sem("log_mm"), sem("log_ready"), sem("lgt_mm"))
        logit_diff_ready, prob_ready = sem("logit_diff_ready"), sem("prob_ready")
        logit_ready, top_ready, index_ready, seen_ready, rank_step, rank_mm, row_step, place_ready = (
            sem("logit_ready"), sem("top_ready"), sem("index_ready"), sem("seen_ready"), sem("rank_step"),
            sem("rank_mm"), sem("row_step"), sem("place_ready"))
        block = ctx.enter_context(nc.Block())
        H2T_0, ACT_0, LOG_0, HIDM_0, LOGM_0, TR_0, H2K_0, H2_0, PL_0 = 2, HC, 1, 2 * HC, 2, 2, 2, 1, 1
        N_RANK = TPB + 4
        N_ROW = 4
        bank_before = lambda hc: hc - HB if hc >= HB else max(
            h for h in range(HC) if h % HB == hc % HB) - HC

        def block_rows(m):
            return rows_sb[:, ds(m * (TPB * PAY), TPB * PAY)].rearrange("p (t d) -> p t d", d=PAY)

        @block.sync
        def _(sp):
            sp.dma_start(out[0:NTOK, :].rearrange("(n p) d -> p n d", p=P),
                         rows_sb[:, :].rearrange("p (n d) -> p n d", d=PAY)[:, :, 0:D]).then_inc(x1_stored, 16)
            w1v = w1[:, :].rearrange("p (e k n) -> p e k n", e=E, k=KC)
            for e in range(E):
                sp.dma_start(w1v[:, e], a["w1"][e].rearrange("(k p) n -> p k n", p=P)).then_inc(w1_in, 16)

        @block.tensor
        def _(pe):
            def step(m, u, active):
                if active(4):
                    pe.wait_ge(log_ready, m - 4 + (LOG_0 + 1))
                    pe.transpose(lgt_ps[:, 0:P], log_sb[:, :], ident[:, :]).then_inc(lgt_mm, 1)
                if active(5):
                    n = m - 5
                    pe.wait_ge(rank_step, n * N_RANK + N_RANK)
                    flat = lambda t: t.rearrange("p t e -> p (t e)")
                    pe.matmul(rank_ps[:, 0:TPB * E], before[:, :], flat(both[:, :, :]), start=True, stop=False)
                    pe.matmul(rank_ps[:, 0:TPB * E], all_ones[:, :], flat(seen[:, 0:TPB, :]),
                              start=False, stop=True).then_inc(rank_mm, 1)
                if active(3):
                    n, p = m - 3, (u - 3) % 2
                    pe.wait_ge(act_ready, n * HC + (HC + ACT_0))
                    pe.wait_ge(log_ready, n + LOG_0)
                    for hc in range(HC):
                        for t in range(TPB):
                            mm = pe.matmul(log_ps[t * LW:(t + 1) * LW, 0:P], rw2[:, hc, :],
                                           act_t[:, p, hc, t * P:(t + 1) * P],
                                           start=(hc == 0), stop=(hc == HC - 1))
                    mm.then_inc(log_mm, 1)
                if active(1):
                    n, p = m - 1, (u - 1) % 2
                    pe.wait_ge(h2_ready, n * TPB + (TPB + H2_0))
                    pe.wait_ge(h2_t_step, n * 2 + H2T_0)
                    for t in range(TPB):
                        for k in range(KC):
                            tr = pe.transpose(tr_ps[:, k, t * P:(t + 1) * P],
                                              h2_blk[:, p, t, k * P:(k + 1) * P], ident[:, :])
                    tr.then_inc(tr_mm, 1)
                if active(2):
                    n, p = m - 2, u % 2
                    pe.wait_ge(h2_t_step, n * 2 + (H2T_0 + 2))
                    for hc in range(HC):
                        pe.wait_ge(act_ready, n * HC + (bank_before(hc) + 1 + ACT_0))
                        terms = [(w, x, k) for w, x in ((rw1_hi, h2_hi), (rw1_hi, h2_lo), (rw1_lo, h2_hi))
                                 for k in range(KC)]
                        for j, (w, x, k) in enumerate(terms):
                            mm = pe.matmul(hid_ps[:, hc % HB, :], w[:, k * HID + hc * P:k * HID + (hc + 1) * P],
                                           x[:, p, k, :], start=(j == 0), stop=(j == len(terms) - 1))
                        mm.then_inc(hid_mm, 1)

            pe.sem_inc(log_mm, LOGM_0)
            pe.sem_inc(tr_mm, TR_0)
            pe.sem_inc(hid_mm, HIDM_0)
            skewed(pe, N_RBLK, 5, 2, step)
            pe.wait_ge(place_ready, N_RBLK + PL_0)
            pe.wait_ge(rank_step, N_RBLK * N_RANK)
            pe.matmul(rank_ps[:, TPB * E:TPB * E + E], all_ones[:, :], seen[:, TPB, :], start=True, stop=True
                      ).then_inc(sums_mm, 1)

        @block.scalar
        def _(act):
            act.sem_inc(act_ready, ACT_0)
            act.sem_inc(h2_kept, H2K_0)
            act.wait_ge(x1_stored, 16)

            def step(m, u, active):
                if active(5):
                    act.wait_ge(logit_diff_ready, m - 5 + 1)
                    act.activation(prob_diff[:, :], logit_diff[:, :], ACT.Tanh, scale=0.5).then_inc(prob_ready, 1)
                if active(2):
                    n, p = m - 2, u % 2
                    act.wait_ge(log_mm, n + (LOGM_0 - 1))
                    for hc in range(HC):
                        act.wait_ge(hid_mm, n * HC + (hc + 1 + HIDM_0))
                        act.activation(act_t[:, p, hc, :], hid_ps[:, hc % HB, :], ACT.Silu,
                                       bias=rb1[:, hc:hc + 1]).then_inc(act_ready, 1)
                if active(0):
                    act.wait_ge(h2_ready, m * TPB + (TPB + H2_0))
                    act.activation(block_rows(m)[:, :, 0:D], h2_blk[:, u % 2, :, :], ACT.Copy).then_inc(h2_kept, 1)

            skewed(act, N_RBLK, 5, 2, step)

        @block.gpsimd
        def _(pool):
            for n in range(N_RBLK):
                pool.wait_ge(h2_kept, n + 1 + H2K_0)
                pool.wait_ge(place_ready, n + 1 + PL_0)
                for t in range(TPB):
                    for s in range(TOPK):
                        tile = n * TPB + t
                        j = tile * TOPK + s
                        pool.indirect_dma_start(dram["x_rows"],
                                                bass.IndirectOffsetOnAxis(ap=place[:, j:j + 1], axis=0),
                                                rows_sb[:, tile * PAY:(tile + 1) * PAY], None).then_inc(scattered, 16)
            pool.wait_ge(pads_ready, 1)
            for e in range(E):
                pool.indirect_dma_start(dram["x_rows"], bass.IndirectOffsetOnAxis(ap=pad_row[:, e:e + 1], axis=0),
                                        blank[:, :], None).then_inc(scattered, 16)
            pool.wait_ge(scattered, 16 * (NTILE * TOPK + E))

        @block.vector
        def _(dve):
            def place_rows(n):
                dve.wait_ge(rank_mm, n + 1)
                dve.tensor_tensor(row[:, :, :], rank_ps[:, 0:TPB * E].rearrange("p (t e) -> p t e", e=E),
                                  region_base[:, :].rearrange("p (o e) -> p o e", o=1).broadcast_to([P, TPB, E]),
                                  ALU.add).then_inc(row_step, 1)
                dve.wait_ge(row_step, n * N_ROW + 1)
                for s in range(TOPK):
                    dve.tensor_tensor(picked[:, :, s, :], hot[:, :, s, :], row[:, :, :], ALU.mult
                                      ).then_inc(row_step, 1)
                dve.wait_ge(row_step, n * N_ROW + 3)
                dve.wait_ge(place_ready, n + PL_0)
                dve.sem_inc(waited, 1)
                dve.tensor_reduce(place_f[:, :], picked[:, :, :, :].rearrange("p t s e -> p (t s) e"), AX_X,
                                  ALU.add).then_inc(row_step, 1)
                dve.wait_ge(prob_ready, n + 1)
                dve.wait_ge(h2_kept, n + (H2K_0 + 1))
                dve.sem_inc(waited, 1)
                rows = block_rows(n)
                dve.tensor_copy(rows[:, :, DIFF_PROB], prob_diff[:, :])
                dve.tensor_scalar(rows[:, :, SECOND_PROB], prob_diff[:, :], -0.5, 0.5, ALU.mult, ALU.add)
                dve.tensor_copy(rows[:, :, FIRST_EXPERT], index_f[:, :, 0])
                dve.wait_ge(row_step, n * N_ROW + 4)
                dve.tensor_copy(place[:, ds(n * SLOTS, SLOTS)], place_f[:, :]).then_inc(place_ready, 1)

            def choose(n):
                dve.wait_ge(lgt_mm, n + 1)
                dve.tensor_tensor(logits[:, :, :], lgt_ps[:, 0:P].rearrange("p (t e) -> p t e", e=LW)[:, :, 0:E],
                                  rb2[:, :].rearrange("p (o e) -> p o e", o=1).broadcast_to([P, TPB, E]),
                                  ALU.add).then_inc(logit_ready, 1)
                dve.wait_ge(logit_ready, n + 1)
                dve.sem_inc(waited, 1)
                for t in range(TPB):
                    dve.max(top8[:, t, :], logits[:, t, :]).then_inc(top_ready, 1)
                dve.wait_ge(top_ready, n * TPB + TPB)
                dve.sem_inc(waited, 1)
                for t in range(TPB):
                    dve.max_index(index8[:, t, :], top8[:, t, :], logits[:, t, :]).then_inc(index_ready, 1)
                dve.wait_ge(index_ready, n * TPB + TPB)
                dve.tensor_tensor(logit_diff[:, :], top8[:, :, 0], top8[:, :, 1], ALU.subtract
                                  ).then_inc(logit_diff_ready, 1)
                dve.tensor_copy(index_f[:, :, :], index8[:, :, 0:TOPK]).then_inc(rank_step, 1)
                dve.wait_ge(rank_step, n * N_RANK + 1)
                dve.tensor_tensor(hot[:, :, :, :].rearrange("p t s e -> p (t s) e"),
                                  index_f[:, :, :].rearrange("p t (s o) -> p (t s) o", o=1
                                                             ).broadcast_to([P, SLOTS, E]),
                                  expert_iota[:, :].rearrange("p (o e) -> p o e", o=1).broadcast_to([P, SLOTS, E]),
                                  ALU.is_equal).then_inc(rank_step, 1)
                dve.tensor_copy(seen[:, 0, :], seen[:, TPB, :]).then_inc(rank_step, 1)
                dve.wait_ge(rank_step, n * N_RANK + 3)
                dve.tensor_tensor(both[:, :, :], hot[:, :, 0, :], hot[:, :, 1, :], ALU.add).then_inc(rank_step, 1)
                for t in range(TPB):
                    dve.wait_ge(rank_step, n * N_RANK + (4 + t))
                    dve.tensor_tensor(seen[:, t + 1, :], seen[:, t, :], both[:, t, :], ALU.add
                                      ).then_inc(rank_step, 1)

            def normalise(m, u):
                dve.wait_ge(tr_mm, m + (TR_0 - 1))
                dve.wait_ge(h2_kept, m + (H2K_0 - 1))
                for t in range(TPB):
                    tile = m * TPB + t
                    mod = m // NBLK * (6 * D)
                    dve.tensor_scalar(xn[:, 0, :], rows_sb[:, ds(tile * PAY, D)], rstd2[:, ds(tile, 1)],
                                      stats2[:, ds(tile * 2, 1)], ALU.mult, ALU.add).then_inc(ln_step, 1)
                    dve.wait_ge(ln_step, tile * 2 + 1)
                    dve.wait_ge(h2_ready, tile + H2_0)
                    dve.tensor_tensor(xn[:, 1, :], xn[:, 0, :], modrow[:, ds(mod + 4 * D, D)],
                                      ALU.mult).then_inc(ln_step, 1)
                    dve.wait_ge(ln_step, tile * 2 + 2)
                    dve.tensor_tensor(h2_blk[:, u % 2, t, :], xn[:, 1, :], modrow[:, ds(mod + 3 * D, D)],
                                      ALU.add).then_inc(h2_ready, 1)

            def step(m, u, active):
                if active(5):
                    place_rows(m - 5)
                if active(4):
                    choose(m - 4)
                if active(3):
                    n = m - 3
                    dve.wait_ge(log_mm, n + (LOGM_0 + 1))
                    dve.tensor_copy(log_sb[:, :], log_ps[:, 0:P]).then_inc(log_ready, 1)
                if active(1):
                    n, p = m - 1, (u - 1) % 2
                    dve.wait_ge(tr_mm, n + (TR_0 + 1))
                    dve.wait_ge(hid_mm, n * HC + (HIDM_0 - HC))
                    dve.tensor_copy(h2_hi[:, p, :, :], tr_ps[:, :, :]).then_inc(h2_t_step, 1)
                    dve.wait_ge(h2_t_step, n * 2 + (H2T_0 + 1))
                    dve.tensor_tensor(h2_lo[:, p, :, :], tr_ps[:, :, :], h2_hi[:, p, :, :].bitcast(F32),
                                      ALU.subtract).then_inc(h2_t_step, 1)
                if active(0):
                    normalise(m, u)

            dve.sem_inc(h2_ready, H2_0)
            dve.sem_inc(h2_t_step, H2T_0)
            dve.sem_inc(log_ready, LOG_0)
            dve.sem_inc(place_ready, PL_0)
            dve.memset(seen[:, :, :], 0.0).then_inc(seen_ready, 1)
            dve.tensor_copy(rows_sb[:, :].rearrange("p (n d) -> p n d", d=PAY)[:, :, TOKEN], token_f[:, 0:NTILE])
            dve.wait_ge(seen_ready, 1)
            skewed(dve, N_RBLK, 5, 2, step)
            done = [0]

            def then_wait(ins):
                done[0] += 1
                ins.then_inc(chain, 1)
                dve.wait_ge(chain, done[0])

            wide = lambda ap, shape: ap.broadcast_to(shape)
            dve.wait_ge(sums_mm, 1)
            dve.tensor_tensor(pad_row[:, :], rank_ps[:, TPB * E:TPB * E + E], pad_base[:, :], ALU.add
                              ).then_inc(pads_ready, 1)
            then_wait(dve.tensor_scalar(count[:, :], rank_ps[:, TPB * E:TPB * E + E], float(P - 1), None, ALU.add))
            then_wait(dve.tensor_copy(count_i[:, :], count[:, :]))
            then_wait(dve.tensor_scalar(count_i[:, :], count_i[:, :], 7, 7, ALU.logical_shift_right,
                                        ALU.logical_shift_left))
            then_wait(dve.tensor_copy(padded[:, :], count_i[:, :]))
            then_wait(dve.tensor_copy(start[:, 0, :], padded[:, :]))
            side = 0
            for d in (1, 2, 4):
                dve.tensor_copy(start[:, 1 - side, 0:d], start[:, side, 0:d])
                then_wait(dve.tensor_tensor(start[:, 1 - side, d:], start[:, side, d:],
                                            start[:, side, 0:E - d], ALU.add))
                side = 1 - side
            ends = start[:, side, :]
            then_wait(dve.tensor_scalar(tile_first[:, :], tile_first[:, :], float(P), None, ALU.mult))
            then_wait(dve.tensor_tensor(passed[:, :, :],
                                        wide(tile_first[:, :].rearrange("p (n o) -> p n o", o=1), [P, NET, E]),
                                        wide(ends.rearrange("p (o e) -> p o e", o=1), [P, NET, E]), ALU.is_ge))
            then_wait(dve.tensor_reduce(expert_f[:, :], passed[:, :, :], AX_X, ALU.add))
            then_wait(dve.tensor_scalar(expert_f[:, :], expert_f[:, :], float(E - 1), None, ALU.min))
            dve.tensor_copy(tile_expert[:, :], expert_f[:, :])
            then_wait(dve.tensor_scalar(skipped[:, :], padded[:, :], -1.0, float(REGION), ALU.mult, ALU.add))
            then_wait(dve.tensor_tensor(passed[:, :, :], passed[:, :, :],
                                        wide(skipped[:, :].rearrange("p (o e) -> p o e", o=1), [P, NET, E]),
                                        ALU.mult))
            then_wait(dve.tensor_reduce(row_f[:, :], passed[:, :, :], AX_X, ALU.add))
            then_wait(dve.tensor_tensor(row_f[:, :], row_f[:, :], tile_first[:, :], ALU.add))
            dve.tensor_scalar(tile_row[:, :], row_f[:, :], float(VOID), None, ALU.min)


def stage_experts(nc, a, dram, modrow, ident, tile_expert, expert_f, tile_row, w1, w1_in, out):
    with ExitStack() as ctx:
        sb = lambda n, s, dt=F32: ctx.enter_context(nc.sbuf_tensor(n, s, dt))
        ps = lambda n, s: ctx.enter_context(nc.psum_tensor(n, s, F32))
        sem = lambda n: ctx.enter_context(nc.semaphore(n))
        HC = HID // P
        w2 = sb("w2", [P, E * HID // P * D])
        b1 = sb("b1", [P, E * HID // P])
        b2 = sb("b2", [P, E * D])
        rows = sb("rows", [P, 2, PAY])
        late = sb("late", [P, TR])
        share = sb("share", [P, 2, TR])
        token = sb("token", [P, TR], U32)
        gate = sb("gate2", [P, D])
        rows_t = sb("rows_t", [P, 2, D])
        hid = sb("hid", [P, 2, HID])
        hid_t = sb("hid_t", [P, 2, HID])
        y = sb("y", [P, 2, D])
        x_tr_ps = ps("x_tr_ps", [P, BLK])
        fc1_ps = ps("fc1_ps", [P, HID])
        h_tr_ps = ps("h_tr_ps", [P, HID])
        fc2_ps = ps("fc2_ps", [P, BLK])
        rows_in = [sem(f"rows_in{p}") for p in range(2)]
        b1_in, w2_in = sem("b1_in"), sem("w2_in")
        added, y_free = sem("added"), sem("y_free")
        gate_diff_ready, gate_ready, y_sum_ready, share_step, meta_ready, waited = (
            sem("gate_diff_ready"), sem("gate_ready3"), sem("y_sum_ready"), sem("share_step"), sem("meta_ready"),
            sem("e_waited"))
        waited_dve = sem("e_waited_dve")
        x_tr_mm, rows_t_ready, fc1_mm, hid_ready, h_tr_mm, hid_t_ready, fc2_mm, y_ready = (
            sem("x_tr_mm"), sem("rows_t_ready"), sem("fc1_mm"), sem("hid_ready"), sem("h_tr_mm"),
            sem("hid_t_ready"), sem("fc2_mm"), sem("y_ready"))
        block = ctx.enter_context(nc.Block())
        XTR_0, RT_0, FC1_0, HID_0, HTR_0, HT_0, FC2_0, YS_0, Y_0, META_0, FREE_0 = 2, 1, 2, 1, 2, 1, 2, 1, TR, 2, TR

        @block.sync
        def _(sp):

            def step(m, u, active):
                if active(0):
                    sp.wait_ge(x_tr_mm, m + (XTR_0 - 1))
                    sp.wait_ge(meta_ready, m + (META_0 - 1))
                    row = sp.value_load(tile_row[0:1, ds(m, 1)], min_val=0, max_val=VOID)
                    sp.dma_start(rows[:, u % 2, :], dram["x_rows"][ds(row, P), :]).then_inc(rows_in[u % 2], 16)

            skewed(sp, NET, 0, 2, step)

        @block.gpsimd
        def _(pool):
            pool.sem_inc(y_free, FREE_0)
            with pool.Fori(0, NET // TR) as i:
                for u in range(TR):
                    n = i * TR + u
                    pool.wait_ge(y_ready, n + (Y_0 + 1))
                    pool.sem_inc(waited, 1)
                    pool.indirect_dma_start(out, bass.IndirectOffsetOnAxis(ap=token[:, u:u + 1], axis=0),
                                            y[:, u % 2, :], None, compute_op=ALU.add).then_inc(added, 16)
                    pool.wait_ge(added, n * 16 + 16)
                    pool.sem_inc(y_free, 1)

        @block.tensor
        def _(pe):
            pe.sem_inc(x_tr_mm, XTR_0)
            pe.sem_inc(fc1_mm, FC1_0)
            pe.sem_inc(h_tr_mm, HTR_0)
            pe.sem_inc(fc2_mm, FC2_0)
            pe.wait_ge(w1_in, 16 * E)

            def expert_of(n):
                return pe.value_load(tile_expert[0:1, ds(n, 1)], min_val=0, max_val=E - 1)

            def step(m, u, active):
                if active(0):
                    pe.wait_ge(rows_in[u % 2], (m // 2) * 16 + 16)
                    pe.wait_ge(rows_t_ready, m + RT_0)
                    for k in range(KC):
                        tr = pe.transpose(x_tr_ps[:, k * P:(k + 1) * P], rows[:, u % 2, k * P:(k + 1) * P],
                                          ident[:, :])
                    tr.then_inc(x_tr_mm, 1)
                if active(1):
                    n, p = m - 1, (u - 1) % 2
                    e = expert_of(n)
                    pe.wait_ge(rows_t_ready, n + (RT_0 + 1))
                    pe.wait_ge(hid_ready, n + HID_0)
                    for half in range(HID // BLK):
                        for k in range(KC):
                            mm = pe.matmul(fc1_ps[:, half * BLK:(half + 1) * BLK], rows_t[:, p, k * P:(k + 1) * P],
                                           w1[:, ds(e * (KC * HID) + (k * HID + half * BLK), BLK)],
                                           start=(k == 0), stop=(k == KC - 1))
                    mm.then_inc(fc1_mm, 1)
                if active(2):
                    n, p = m - 2, u % 2
                    pe.wait_ge(hid_ready, n + (HID_0 + 1))
                    pe.wait_ge(hid_t_ready, n + HT_0)
                    for hc in range(HC):
                        tr = pe.transpose(h_tr_ps[:, hc * P:(hc + 1) * P], hid[:, p, hc * P:(hc + 1) * P],
                                          ident[:, :])
                    tr.then_inc(h_tr_mm, 1)
                if active(3):
                    n, p = m - 3, (u - 3) % 2
                    e = expert_of(n)
                    if isinstance(n, int) and n == 0:
                        pe.wait_ge(w2_in, 16 * (E + 1))
                    pe.wait_ge(hid_t_ready, n + (HT_0 + 1))
                    pe.wait_ge(y_sum_ready, n + YS_0)
                    for hc in range(HC):
                        mm = pe.matmul(fc2_ps[:, 0:D], hid_t[:, p, hc * P:(hc + 1) * P],
                                       w2[:, ds(e * (HC * D) + hc * D, D)], start=(hc == 0), stop=(hc == HC - 1))
                    mm.then_inc(fc2_mm, 1)

            skewed(pe, NET, 3, 2, step)

        @block.scalar
        def _(act):
            act.sem_inc(hid_t_ready, HT_0)
            act.dma_start(b1[:, :], a["b1_cols"]).then_inc(b1_in, 16)
            w2v = w2[:, :].rearrange("p (e c n) -> p e c n", e=E, c=HID // P)
            for e in range(E):
                act.dma_start(w2v[:, e], a["w2"][e].rearrange("(c p) n -> p c n", p=P)).then_inc(w2_in, 16)
            act.dma_start(b2[:, :], a["b2"].partition_broadcast(P)).then_inc(w2_in, 16)
            act.wait_ge(b1_in, 16)

            def step(m, u, active):
                if active(2):
                    n, p = m - 2, u % 2
                    act.wait_ge(h_tr_mm, n + (HTR_0 + 1))
                    act.wait_ge(fc2_mm, n + (FC2_0 - 1))
                    e = act.value_load(tile_expert[0:1, ds(n, 1)], min_val=0, max_val=E - 1)
                    for hc in range(HC):
                        cols = slice(hc * P, (hc + 1) * P)
                        silu = act.activation(hid_t[:, p, cols], h_tr_ps[:, cols], ACT.Silu,
                                              bias=b1[:, ds(e * HC + hc, 1)])
                    silu.then_inc(hid_t_ready, 1)

            skewed(act, NET, 2, 2, step)

        @block.vector
        def _(dve):
            dve.sem_inc(rows_t_ready, RT_0)
            dve.sem_inc(hid_ready, HID_0)
            dve.sem_inc(y_sum_ready, YS_0)
            dve.sem_inc(y_ready, Y_0)
            dve.sem_inc(meta_ready, META_0)
            gates = [modrow[:, (6 * b + 5) * D:(6 * b + 6) * D] for b in range(B)]
            dve.tensor_tensor(gates[1], gates[1], gates[0], ALU.subtract).then_inc(gate_diff_ready, 1)
            dve.wait_ge(gate_diff_ready, 1)

            def expert_of(n):
                return dve.value_load(tile_expert[0:1, ds(n, 1)], min_val=0, max_val=E - 1)

            def step(m, u, active):
                if active(0):
                    dve.wait_ge(x_tr_mm, m + (XTR_0 + 1))
                    dve.wait_ge(fc1_mm, m + (FC1_0 - 1))
                    dve.tensor_copy(rows_t[:, u % 2, :], x_tr_ps[:, 0:D]).then_inc(rows_t_ready, 1)
                if active(1):
                    n, p = m - 1, (u - 1) % 2
                    dve.wait_ge(fc1_mm, n + (FC1_0 + 1))
                    dve.wait_ge(h_tr_mm, n + (HTR_0 - 1))
                    dve.tensor_copy(hid[:, p, :], fc1_ps[:, :]).then_inc(hid_ready, 1)
                if active(3):
                    n, p, k = m - 3, (u - 3) % 2, (u - 3) % TR
                    e = expert_of(n)
                    dve.wait_ge(y_ready, n + Y_0)
                    dve.scalar_tensor_tensor(gate[:, :], gates[1], late[:, k:k + 1], gates[0],
                                             ALU.mult, ALU.add).then_inc(gate_ready, 1)
                    dve.wait_ge(fc2_mm, n + (FC2_0 + 1))
                    dve.wait_ge(y_free, n + (FREE_0 - 1))
                    dve.tensor_tensor(y[:, p, :], fc2_ps[:, 0:D], b2[:, ds(e * D, D)], ALU.add
                                      ).then_inc(y_sum_ready, 1)
                    dve.wait_ge(gate_ready, n + 1)
                    dve.wait_ge(y_sum_ready, n + (YS_0 + 1))
                    dve.scalar_tensor_tensor(y[:, p, :], y[:, p, :], share[:, 1, k:k + 1], gate[:, :],
                                             ALU.mult, ALU.mult).then_inc(y_ready, 1)
                if active(0):
                    k = u % TR
                    col = lambda c: rows[:, u % 2, c:c + 1]
                    dve.wait_ge(rows_in[u % 2], (m // 2) * 16 + 16)
                    dve.wait_ge(y_ready, m + (Y_0 - TR + 1))
                    dve.wait_ge(y_free, m + (FREE_0 - TR + 1))
                    dve.sem_inc(waited_dve, 1)
                    dve.tensor_scalar(late[:, k:k + 1], col(TOKEN), float(T), None, ALU.is_ge)
                    dve.tensor_copy(token[:, k:k + 1], col(TOKEN))
                    dve.tensor_scalar(share[:, 0, k:k + 1], col(FIRST_EXPERT), expert_f[:, ds(m, 1)],
                                      col(DIFF_PROB), ALU.is_equal, ALU.mult).then_inc(share_step, 1)
                    dve.wait_ge(share_step, m + 1)
                    dve.tensor_tensor(share[:, 1, k:k + 1], share[:, 0, k:k + 1], col(SECOND_PROB), ALU.add
                                      ).then_inc(meta_ready, 1)

            skewed(dve, NET, 3, TR, step)


INPUTS = ["x", "c_t", "wmod", "ident", "scalars", "transforms", "transform_weights", "qkv_wt", "code_wt",
          "head_sum", "soft_sum", "out_wt", "rw1", "rw2", "rb1_cols", "rb2", "before", "ones", "iota",
          "region_base", "pad_base", "token_rows",
          "w1", "w2", "b1_cols", "b2"]


def kernel(**inputs):
    import numpy as np
    import concourse.bacc as bacc
    from concourse.bass_utils import run_bass_kernel_spmd

    arr = lambda name: np.asarray(inputs["L0_" + name])
    flat = np.ascontiguousarray
    scalars = [arr("attn_hamming_lambda_logit"), arr("attn_scale_logit"), arr("attn_sips_alpha"),
               arr("attn_sips_beta")]
    given = {
        "x": flat(arr("attn_x").reshape(NTOK, D)),
        "c_t": flat(arr("c").T),
        "wmod": flat(arr("wmod")),
        "scalars": np.concatenate([s.reshape(1) for s in scalars]),
        "transforms": flat(arr("attn_transforms").transpose(1, 0, 2)),
        "transform_weights": flat(arr("attn_transform_weights").reshape(H * NT)),
        "qkv_wt": flat(arr("attn_qkv_w").T),
        "code_wt": flat(np.concatenate([arr("attn_q6_w"), arr("attn_hex_w")]).T),
        "out_wt": flat(arr("attn_out_w").T),
        "rw1": flat(arr("ffn_rw1")),
        "rw2": flat(arr("ffn_rw2")),
        "rb1_cols": flat(arr("ffn_rb1").reshape(HID // P, P).T),
        "rb2": flat(arr("ffn_rb2")),
        "w1": flat(arr("ffn_w1")),
        "w2": flat(arr("ffn_w2")),
        "b1_cols": flat(arr("ffn_b1").reshape(E * HID // P, P).T),
        "b2": flat(arr("ffn_b2").reshape(E * D)),
        "ident": np.eye(P, dtype=np.float32),
        "head_sum": np.repeat(np.eye(H, dtype=np.float32), HEX, axis=0),
        "soft_sum": np.repeat(np.array([[0.0], [1.0]], np.float32), HEX, axis=0).repeat(H, axis=1),
        "before": np.triu(np.ones((P, P), np.float32), 1),
        "ones": np.ones((P, P), np.float32),
        "iota": np.arange(NET, dtype=np.float32),
        "region_base": np.arange(E, dtype=np.float32) * REGION,
        "token_rows": (np.arange(P)[:, None] + np.arange(NTILE + 1)[None, :] * P).astype(np.float32),
        "pad_base": (np.arange(P)[:, None] + np.arange(E)[None, :] * REGION).astype(np.float32),
    }
    nc = bacc.Bacc("TRN2", target_bir_lowering=False, num_devices=1)
    arrays = {f"in_{name}": given[name] for name in INPUTS}
    a = {name: nc.dram_tensor(f"in_{name}", given[name].shape, F32, kind="ExternalInput").ap() for name in INPUTS}
    out = nc.dram_tensor("out", (NTOK + P, D), F32, kind="ExternalOutput").ap()
    build(nc, a, out)
    r = run_bass_kernel_spmd(nc, [arrays], core_ids=[0])
    return r.results[0]["out"][:NTOK].reshape(B, T, D)
```
